# Optimizing a Trainium2 kernel written in Bass

```python
import numpy as np
import jax
import jax.numpy as jnp

def _softmax(x, axis=-1):
    return jax.nn.softmax(x, axis=axis)

def _gelu(x):
    return jax.nn.gelu(x, approximate=True)

def _silu(x):
    return jax.nn.silu(x)

def _sigmoid(x):
    return jax.nn.sigmoid(x)

def _layernorm(x, axis=-1, eps=1e-05):
    m = jnp.mean(x, axis=axis, keepdims=True)
    v = jnp.var(x, axis=axis, keepdims=True)
    return (x - m) / jnp.sqrt(v + eps)

def _scatter_add(tgt, idx, src, axis=0):
    return tgt.at[idx].add(src)

def _segment_sum(src, seg, n):
    return jax.ops.segment_sum(src, seg, n)
kernel_name = 'mk_adj_preln_d2_adj_r2_09c14d'

def setup_inputs(seed: int=0):
    np.random.seed(seed)
    _w = jnp.asarray

    def _rec_inputs():
        import jax
        import jax.numpy as jnp
        _gk = jax.random.key(seed)
        x = -9.806e-05 + 1 * jax.random.normal(jax.random.fold_in(_gk, 1), (4096, 128), jnp.float32)
        _w = (1.0 + jnp.arange(4096, dtype=jnp.float32)) ** (-0.5)
        _w = _w / _w.mean()
        _pij = jnp.clip(0.00195312 * _w[:, None] * _w[None, :], 0.0, 1.0)
        _a = jax.random.uniform(jax.random.fold_in(_gk, 2), (4096, 4096)) < _pij
        _a = jnp.logical_or(_a, jnp.eye(4096, dtype=bool))
        _af = _a.astype(jnp.float32)
        _af = _af * jax.random.uniform(jax.random.fold_in(_gk, 3), (4096, 4096), jnp.float32, 0.05, 1)
        adj = _af
        return (x, adj)
    x, adj = _rec_inputs()

    def _L0_gnn_setup():
        import jax, jax.numpy as jnp
        import numpy as np

        def _lap_mul(A, x):
            d = 1.0 / jnp.sqrt(jnp.sum(A, axis=-1))
            return d[:, None] * (A @ (d[:, None] * x))
        key = jax.random.key(seed)
        k1, k2, k3, k4, k5, k6 = jax.random.split(key, 6)
        N, D_IN, D_OUT = (2048, 128, 128)
        x = jax.random.normal(k1, (N, D_IN), dtype=jnp.float32)
        A = jax.random.uniform(k2, (N, N), dtype=jnp.float32)
        s1 = 1.0 / np.sqrt(D_IN)
        W1 = jax.random.uniform(k3, (D_IN, D_OUT), minval=-s1, maxval=s1, dtype=jnp.float32)
        b1 = jax.random.uniform(k4, (D_OUT,), minval=-s1, maxval=s1, dtype=jnp.float32)
        W2 = jax.random.uniform(k5, (D_IN, D_OUT), minval=-s1, maxval=s1, dtype=jnp.float32)
        b2 = jax.random.uniform(k6, (D_OUT,), minval=-s1, maxval=s1, dtype=jnp.float32)
        return {'x': x, 'A': A, 'W1': W1, 'b1': b1, 'W2': W2, 'b2': b2, 'sigma': 1, 'k': 4}
    _L0_gnn_all = _L0_gnn_setup()
    _L0_gnn_in = {k: v for k, v in _L0_gnn_all.items() if k in ('W1', 'b1', 'W2', 'b2')}
    del _L0_gnn_all

    def _L1_gnn_setup():
        import jax, jax.numpy as jnp
        import numpy as np
        N, IN_F, OUT_F = (4096, 128, 128)
        key = jax.random.key(seed)
        k1, k2, k3 = jax.random.split(key, 3)
        x = jax.random.normal(k1, (N, IN_F), dtype=jnp.float32)
        adj = jax.random.uniform(k2, (N, N), dtype=jnp.float32)
        limit = np.sqrt(6.0 / (IN_F + OUT_F)).astype(np.float32)
        weight = jax.random.uniform(k3, (IN_F, OUT_F), dtype=jnp.float32, minval=-limit, maxval=limit)
        return {'x': x, 'adj': adj, 'weight': weight}
    _L1_gnn_all = _L1_gnn_setup()
    _L1_gnn_in = {k: v for k, v in _L1_gnn_all.items() if k in ('weight',)}
    del _L1_gnn_all
    return {'x': x, 'adj': adj, 'L0_gnn_W1': _L0_gnn_in['W1'], 'L0_gnn_b1': _L0_gnn_in['b1'], 'L0_gnn_W2': _L0_gnn_in['W2'], 'L0_gnn_b2': _L0_gnn_in['b2'], 'L1_gnn_weight': _L1_gnn_in['weight']}

def reference(x, adj, L0_gnn_W1, L0_gnn_b1, L0_gnn_W2, L0_gnn_b2, L1_gnn_weight):
    import jax
    import jax.numpy as jnp

    def _L0_gnn_ref(x, A, W1, b1, W2, b2, sigma, k):
        import jax, jax.numpy as jnp
        import numpy as np

        def _lap_mul(A, x):
            d = 1.0 / jnp.sqrt(jnp.sum(A, axis=-1))
            return d[:, None] * (A @ (d[:, None] * x))
        z = _lap_mul(A, x) @ W1 + b1
        z = jax.nn.leaky_relu(z, negative_slope=0.1)
        sq = jnp.sum(z * z, axis=-1)
        d2 = sq[:, None] + sq[None, :] - 2.0 * (z @ z.T)
        d2 = jnp.maximum(d2, 0.0)
        S = jnp.sqrt(d2 + 1e-10)
        S = jnp.exp(-S / (2.0 * sigma))
        order = jnp.argsort(-S, axis=-1)
        ranks = jnp.argsort(order, axis=-1)
        S = jnp.where(ranks < k, S, 0.0)
        A2 = S + A
        out = _lap_mul(A2, x) @ W2 + b2
        return out

    def _L1_gnn_ref(x, adj, weight):
        import jax, jax.numpy as jnp
        import numpy as np
        N, IN_F, OUT_F = (4096, 128, 128)
        degree = jnp.sum(adj, axis=1)
        d_is = degree ** (-0.5)
        normalized_adj = d_is[:, None] * adj * d_is[None, :]
        support = x @ weight
        out = normalized_adj @ support
        return out
    h = jnp.maximum(_layernorm(x, axis=-1), 0.0)
    x = x + _L0_gnn_ref(h, adj, L0_gnn_W1, L0_gnn_b1, L0_gnn_W2, L0_gnn_b2, 1, 4)
    h = jnp.maximum(_layernorm(x, axis=-1), 0.0)
    x = x + _L1_gnn_ref(h, adj, L1_gnn_weight)
    return x

_drawn_inputs = setup_inputs


def setup_inputs(seed=0):
    import zlib

    import numpy as np

    out = dict(_drawn_inputs(seed))
    spreads = {}
    factors = {}
    for name, (base, spread) in spreads.items():
        noise = np.random.default_rng([zlib.crc32(name.encode()), seed]).standard_normal(out[name].shape)
        drawn = base * np.exp(spread * noise) if base else spread * noise
        out[name] = jnp.asarray(drawn.astype(out[name].dtype))
    for name, factor in factors.items():
        out[name] = (out[name] * factor).astype(out[name].dtype)
    return out
```

```python
from contextlib import ExitStack

import concourse.bass as bass
from concourse import mybir

F32 = mybir.dt.float32
F32R = mybir.dt.float32r
BF16 = mybir.dt.bfloat16
U32 = mybir.dt.uint32
ALU = mybir.AluOpType
ACT = mybir.ActivationFunctionType
AX_X = mybir.AxisListType.X
ds = bass.ds

P = 128
N = 4096
D = 128
CH = 512
NC = N // CH
SUB = CH // P
NR = N // P
HALF = SUB // 2 * CH
K = 4
EPS = 1e-5
SLOPE = 0.1

SLOTS = 12
RING = NC
SCH = 2
GRP = 8

DROPPED = {(r, 7) for r in range(7)} | {(r, 6) for r in range(5)} | {(r, 5) for r in range(2)}


def plan_phase_a():
    rows = [(R, J) for R in range(NC) for J in range(R)]
    cols = [(r, J) for J in range(NC) for r in range(J + 1)]
    loads, sums = [], 0
    for R in range(NC):
        order = [(R, J, True) for J in range(R, NC)]
        again = [(r, R, False) for r in range(R) if (r, R) in DROPPED]
        fresh = [(R, J, True) for J in range(R)]
        order += again + fresh if R < NC - 1 else fresh + again
        for r, J, first in order:
            sums += first
            ld = dict(r=r, J=J, reduced=sums if first else 0, row=0, col=0)
            if first and (r, J) in DROPPED:
                ld["key"] = (R, 0, J)
            elif J < r:
                ld["row"] = rows.index((r, J)) + 1
                ld["key"] = (r, 1, J)
            else:
                ld["col"] = cols.index((r, J)) + 1
                ld["key"] = (J, 2, r)
            loads.append(ld)
    owner, count = [None] * SLOTS, [0] * SLOTS
    for ld in loads:
        s = min(range(SLOTS), key=lambda i: (-1,) if owner[i] is None else owner[i]["key"])
        ld["slot"], ld["before"] = s, owner[s]
        owner[s] = ld
        count[s] += 1
        ld["landed"] = 16 * count[s]
    return loads


LOADS = plan_phase_a()
SUMMED = [ld for ld in LOADS if ld["reduced"]]
ROWBLK = {(ld["r"], ld["J"]): ld for ld in LOADS if ld["row"]}
COLBLK = {(ld["r"], ld["J"]): ld for ld in LOADS if ld["col"]}
N_ROW, N_COL = len(ROWBLK), len(COLBLK)
A_HALVES = 2 * N_COL
C_CHUNKS = NC - SCH
C_HALVES = 2 * NC * C_CHUNKS


def build(nc, x, at, w1, b1, w2, b2, w3, out):
    with ExitStack() as ctx:
        def sb(name, shape, dt=F32, stack=ctx):
            return stack.enter_context(nc.sbuf_tensor(name, shape, dt))

        def sem(name):
            return ctx.enter_context(nc.semaphore(name))

        h = sb("h", [P, NR, D])
        ut = sb("ut", [P, 2, CH])
        zt = sb("zt", [P, 2, SUB, D])
        negsq = sb("negsq", [P, N], BF16)
        x2s = sb("x2s", [P, GRP, D])
        zslot = sb("zslot", [P, 2, 2, P], F32R)
        w1s, w2s, w3s = (sb(n, [D, D]) for n in ("w1s", "w2s", "w3s"))
        b1s, b2s = sb("b1s", [P, D]), sb("b2s", [P, D])
        ident = sb("ident", [P, P])
        ident16 = sb("ident16", [P, P], BF16)
        ones16 = sb("ones16", [P, P], BF16)
        ones = sb("ones", [P, 1])
        neghalf = sb("neghalf", [P, NR])
        poshalf = sb("poshalf", [P, K])
        stats = sb("stats", [P, NR, 6])
        meanvar = sb("meanvar", [P, NR, 2])
        vareps = sb("vareps", [P, NR])
        rstd = sb("rstd", [P, NR])
        negmean = sb("negmean", [P, NR])
        shift = sb("shift", [P, NR])
        deg = sb("deg", [P, NR])
        dis = sb("dis", [P, NR])
        sq = sb("sq", [P, NR])
        sqv = sb("sqv", [P, 3, NR])
        sqp = sb("sqp", [P, 3, NR], BF16)
        dis2 = sb("dis2", [P, NR])
        s4 = sb("s4", [P, NR, K])
        idx = sb("idx", [P, NR, K], U32)
        top = sb("top", [P, GRP, 8])
        topi = sb("topi", [P, GRP, 8], U32)
        dist = sb("dist", [P, GRP, 4, K])
        ssum = sb("ssum", [P, GRP])
        deg2 = sb("deg2", [P, GRP])
        idxs = sb("idxs", [P, SUB, K], U32)
        lnstat = sb("lnstat", [P, SUB, 6])
        lnmv = sb("lnmv", [P, SUB, 2])
        lnsc = sb("lnsc", [P, 5, SUB])

        with ExitStack() as a:
            xp = sb("xp", [P, NR, D], F32, a)
            part = sb("part", [P, NC, CH], F32, a)
            xst = sb("xst", [P, 2, 2, CH], F32R, a)
            split_a = sb("split_a", [P, 2, 2, HALF], F32R, a)
            blk = sb("blk", [P, SLOTS, SUB, CH], F32, a)
        pan = [sb("pan_hi", [P, N], F32R), sb("pan_lo", [P, N], F32R)]
        x2p = [sb("x2_hi", [P, N], F32R), sb("x2_lo", [P, N], F32R)]
        ring = sb("ring", [P, RING, SUB, CH])
        with ExitStack() as s:
            score = sb("score", [P, 2, N], F32, s)
        split_d = sb("split_d", [P, 2, 2, HALF], F32R)
        xb = sb("xb", [P, NR, D])
        xg = negsq[:, :].bitcast(F32).rearrange("p (q k f) -> p q k f", q=SUB, k=K)

        ps = ctx.enter_context(nc.psum_tensor("ps", [P, NC, CH], F32))
        x2d = nc.dram_tensor("x2_rows", (N, D), F32, kind="Internal").ap()

        x_in, w_in, b_in, xb_in = (sem(n) for n in ("x_in", "w_in", "b_in", "xb_in"))
        blk_in = [sem(f"blk_in{i}") for i in range(SLOTS)]
        ring_in = [sem(f"ring_in{i}") for i in range(RING)]
        consts, ident_z, ident_ok = sem("consts"), sem("ident_z"), sem("ident_ok")
        stats_ok, mv_ok, ln_step, ln_ok, h_ok = (sem(n) for n in ("stats_ok", "mv_ok", "ln_step", "ln_ok", "h_ok"))
        summed, deg_mm, deg_ok, dis_ok = (sem(n) for n in ("summed", "deg_mm", "deg_ok", "dis_ok"))
        xp_ok, xhi_ok, xlo_ok = (sem(n) for n in ("xp_ok", "xhi_ok", "xlo_ok"))
        hi_made, lo_made, split_used = (sem(n) for n in ("hi_made", "lo_made", "split_used"))
        row_done, chunk1_done = sem("row_done"), sem("chunk1_done")
        u_ok, zw_mm, zt_part, z_ok, sq_ok = (sem(n) for n in ("u_ok", "zw_mm", "zt_part", "z_ok", "sq_ok"))
        zt_mm, zhi_ok, zlo_ok, sqv_ok, sqp_mm, negsq_ok = (
            sem(n) for n in ("zt_mm", "zhi_ok", "zlo_ok", "sqv_ok", "sqp_mm", "negsq_ok"))
        zslot_ok, zz_mm, score_ok, top_ok, topi_ok = (
            sem(n) for n in ("zslot_ok", "zz_mm", "score_ok", "top_ok", "topi_ok"))
        dist_ok, s4_ok, deg2_ok, dis2_ok, x2_ok, x2hi_ok, x2lo_ok, x2_out, x2_used, idx_ok = (
            sem(n) for n in ("dist_ok", "s4_ok", "deg2_ok", "dis2_ok", "x2_ok", "x2hi_ok", "x2lo_ok",
                             "x2_out", "x2_used", "idx_ok"))
        idxs_ok, gathered, weighed, g_mm = sem("idxs_ok"), [sem(f"gathered{q}") for q in range(SUB)], sem("weighed"), sem("g_mm")
        chunk2_done, v_ok, w2_mm, x1_ok, lnst_ok, lnmv_ok, lnsc_ok, x3_ok, x3hi_ok, x3lo_ok, xb_ok = (
            sem(n) for n in ("chunk2_done", "v_ok", "w2_mm", "x1_ok", "lnst_ok", "lnmv_ok", "lnsc_ok",
                             "x3_ok", "x3hi_ok", "x3lo_ok", "xb_ok"))
        chunk3_done, t_ok, w3_mm, y_ok = (sem(n) for n in ("chunk3_done", "t_ok", "w3_mm", "y_ok"))
        waited = sem("waited")
        y_sent = [sem("y_sent0"), sem("y_sent1")]

        def wait_apart(eng, signal, value):
            eng.wait_ge(signal, value)
            eng.sem_inc(waited)

        block = ctx.enter_context(nc.Block())

        @block.sync
        def _(sp):
            sp.dma_start(xp[:, :, :], x[:, :, :]).then_inc(x_in, 16)

            for n, ld in enumerate(LOADS):
                old = ld["before"]
                if n == 2:
                    for dst, src in ((w1s, w1), (w2s, w2), (w3s, w3)):
                        sp.dma_start(dst[:, :], src[:, :]).then_inc(w_in, 16)
                    for dst, src in ((b1s, b1), (b2s, b2)):
                        sp.dma_start(dst[:, :], src.rearrange("(a f) -> a f", a=1).broadcast_to([P, D])).then_inc(b_in, 16)
                if old is not None:
                    if old["reduced"]:
                        sp.wait_ge(summed, old["reduced"])
                    if old["row"]:
                        sp.wait_ge(row_done, old["row"])
                    if old["col"]:
                        sp.wait_ge(lo_made, 2 * old["col"])
                sp.dma_start(blk[:, ld["slot"], :, :], at[ld["r"], ld["J"]]).then_inc(blk_in[ld["slot"]], 16)

            sp.wait_ge(lo_made, A_HALVES)
            sp.wait_ge(split_used, A_HALVES)

            def load_s(J, half):
                for c in range(SCH):
                    slot = SUB + 2 * half + c
                    sp.dma_start(ring[:, slot, :, :], at[c, J]).then_inc(ring_in[slot], 16)

            load_s(0, 0)
            load_s(1, 1)
            for J in range(SUB):
                sp.dma_start(ring[:, J, :, :], at[SCH, J]).then_inc(ring_in[J], 16)
            with sp.Fori(0, NC // 2 - 1) as it:
                for half in range(2):
                    sp.wait_ge(x2_used, it * GRP + SUB * (half + 1))
                    for c in range(SCH):
                        slot = SUB + 2 * half + c
                        sp.dma_start(ring[:, slot, :, :], at[c, ds(it * 2 + (2 + half), 1)].rearrange(
                            "a p s c -> (a p) s c")).then_inc(ring_in[slot], 16)
            for half in range(2):
                sp.wait_ge(x2_used, NR - SUB * (2 - half) + SUB)
                for c in range(SCH):
                    slot = SUB + 2 * half + c
                    sp.dma_start(ring[:, slot, :, :], at[SCH, slot]).then_inc(ring_in[slot], 16)
            sp.wait_ge(topi_ok, NR)
            sp.dma_start(xb[:, :, :], x[:, :, :]).then_inc(xb_in, 16)
            with sp.Fori(1, C_CHUNKS) as k:
                for J in range(NC):
                    sp.wait_ge(lo_made, k * (2 * NC) + (A_HALVES - 2 * NC + 2 * J + 2))
                    sp.dma_start(ring[:, J, :, :], at[ds(k + SCH, 1), J].rearrange(
                        "a p s c -> (a p) s c")).then_inc(ring_in[J], 16)
            with sp.Fori(0, NC) as k:
                for J in range(NC):
                    sp.wait_ge(lo_made, k * (2 * NC) + (A_HALVES + C_HALVES - 2 * NC + 2 * J + 2))
                    sp.dma_start(ring[:, J, :, :], at[ds(k, 1), J].rearrange(
                        "a p s c -> (a p) s c")).then_inc(ring_in[J], 16)
            sp.wait_ge(y_sent[0], 16 * NC // 2)
            sp.wait_ge(y_sent[1], 16 * NC // 2)

        def ring_landed(eng, J, loads_before):
            base = NC // 2 if J >= SUB else 0
            eng.wait_ge(ring_in[J], loads_before * 16 + 16 * (base + 1))

        @block.tensor
        def _(pe):
            def split_half(bank, n, hf, w, wcol, first, last):
                buf = split_a if isinstance(n, int) and n < A_HALVES else split_d
                for sub in range(SUB // 2):
                    c0 = wcol + (hf * (SUB // 2) + sub) * P
                    for g, (wi, ai) in enumerate(((0, 0), (1, 0), (0, 1))):
                        mm = pe.matmul(ps[:, bank, :] if isinstance(bank, int) else
                                       ps[:, ds(bank, 1), :].rearrange("p a c -> p (a c)"),
                                       w[wi][:, c0:c0 + P],
                                       buf[:, hf, ai, sub * CH:(sub + 1) * CH],
                                       start=first and sub == 0 and g == 0,
                                       stop=last and sub == SUB // 2 - 1 and g == 2, skip_group_check=True)
                return mm

            def deg_sum(R):
                pe.wait_ge(summed, NC * (R + 1))
                pe.wait_ge(consts, 1)
                for q in range(SUB):
                    for J in range(NC):
                        mm = pe.matmul(ps[:, NC - 1, R * SUB + q:R * SUB + q + 1], part[:, J, q * P:(q + 1) * P],
                                       ones[:, :], start=(J == 0), stop=(J == NC - 1), skip_group_check=True)
                mm.then_inc(deg_mm, 1)

            def row_block(R, J):
                ld = ROWBLK[R, J]
                pe.wait_ge(blk_in[ld["slot"]], ld["landed"])
                pe.wait_ge(xp_ok, SUB * (J + 1))
                for sub in range(SUB):
                    mm = pe.matmul(ps[:, R, :], xp[:, J * SUB + sub, :], blk[:, ld["slot"], sub, :],
                                   start=(J == 0 and sub == 0), stop=False, skip_group_check=True)
                mm.then_inc(row_done, 1)

            def col_block(r, J):
                ld = COLBLK[r, J]
                if r == 0:
                    pe.wait_ge(xlo_ok, J + 1)
                for hf in range(2):
                    n = 2 * (ld["col"] - 1) + hf
                    pe.wait_ge(lo_made, n + 1)
                    split_half(r, n, hf, [xst[:, J % 2, 0, :], xst[:, J % 2, 1, :]], 0,
                               J == 0 and hf == 0, J == NC - 1 and hf == 1).then_inc(split_used, 1)

            def z_rows(c):
                pe.wait_ge(u_ok, c + 1)
                pe.wait_ge(w_in, 48)
                for q in range(SUB):
                    mm = pe.matmul(ps[:, c, q * D:(q + 1) * D], ut[:, c % 2, q * P:(q + 1) * P], w1s[:, :],
                                   start=True, stop=True, skip_group_check=True)
                mm.then_inc(zw_mm, 1)

            def z_turn(c):
                pe.wait_ge(z_ok, c + 1)
                for q in range(SUB):
                    mm = pe.transpose(ps[:, c, q * P:(q + 1) * P], zt[:, c % 2, q, :], ident[:, :])
                mm.then_inc(zt_mm, 1)

            for R in range(NC):
                if R == NC - 1:
                    deg_sum(R)
                    pe.wait_ge(deg_ok, NC)
                for J in range(R):
                    if R < NC - 1 and J == max(R - 2, 0):
                        deg_sum(R)
                    row_block(R, J)
                if R == 0:
                    deg_sum(0)
                for r in range(R + 1):
                    col_block(r, R)
                    if R == NC - 1:
                        if r == 0:
                            pe.wait_ge(ident_ok, 1)
                        if r >= 1:
                            z_rows(r - 1)
                        if r >= 3:
                            z_turn(r - 3)
            z_turn(NC - 3)
            z_rows(NC - 1)
            z_turn(NC - 2)
            z_turn(NC - 1)
            pe.wait_ge(sqv_ok, 6)
            pe.wait_ge(ident_ok, 2)
            for r in range(NR):
                c = r // SUB
                if r % SUB == 0:
                    pe.wait_ge(zlo_ok, c + 1)
                mm = pe.matmul(ps[0:3, c, (r % SUB) * P:(r % SUB + 1) * P], sqp[:, :, r], ident16[:, :],
                               start=True, stop=True, skip_group_check=True)
                if r % (2 * SUB) == 2 * SUB - 1:
                    mm.then_inc(sqp_mm, 1)

            def zz(r, u):
                pe.wait_ge(zslot_ok, 2 * r + 2)
                for q in range(4):
                    unit = r * 4 + q
                    if not (isinstance(r, int) and r == 0 and q < 2):
                        pe.wait_ge(score_ok, unit - 1)
                    for b in range(2):
                        bank = 4 + 2 * (q % 2) + b
                        cols = slice((2 * q + b) * CH, (2 * q + b + 1) * CH)
                        pe.matmul(ps[:, bank, :], ones16[:, :], negsq[:, cols], start=True, stop=False)
                        for g, (wi, mi) in enumerate(((0, 0), (1, 0), (0, 1))):
                            mm = pe.matmul(ps[:, bank, :], zslot[:, u % 2, wi, :], pan[mi][:, cols],
                                           start=False, stop=(g == 2))
                    mm.then_inc(zz_mm, 1)

            def product_s(r, u, it):
                if u % SUB == 0:
                    for c in range(SCH):
                        slot = SUB + 2 * (u // SUB) + c
                        pe.wait_ge(ring_in[slot], it * 16 + 16)
                pe.wait_ge(x2_ok, r + 1)
                for c in range(SCH):
                    mm = pe.matmul(ps[:, c, :], x2s[:, u, :], ring[:, SUB + 2 * (u // SUB) + c, u % SUB, :],
                                   start=isinstance(r, int) and r == 0, stop=False, skip_group_check=True)
                mm.then_inc(x2_used, 1)

            pe.wait_ge(negsq_ok, 4)
            pe.wait_ge(consts, 1)
            zz(0, 0)
            zz(1, 1)
            for u in range(GRP):
                zz(u + 2, u)
                product_s(u, u, 0)
            with pe.Fori(1, NR // GRP - 1) as it:
                for u in range(GRP):
                    zz(it * GRP + (u + 2), u)
                    product_s(it * GRP + u, u, it)
            for u in range(GRP):
                r = NR - GRP + u
                if r + 2 < NR:
                    zz(r + 2, u)
                product_s(r, u, NR // GRP - 1)

            def product(bank, n0, panels, J):
                for hf in range(2):
                    pe.wait_ge(lo_made, n0 + (2 * J + hf + 1))
                    mm = split_half(bank, n0, hf, panels, J * CH, J == 0 and hf == 0, False)
                    mm.then_inc(split_used, 1)
                return mm

            def bank_of(c):
                return ps[:, c, :] if isinstance(c, int) else ps[:, ds(c, 1), :].rearrange("p a c -> p (a c)")

            def add_neighbours(c):
                for q in range(SUB):
                    pe.wait_ge(weighed, c * (4 * SUB) + 4 * (q + 1))
                    mm = pe.matmul(bank_of(c)[:, q * P:(q + 1) * P], xg[:, q, 0, :], ident[:, :],
                                   start=False, stop=(q == SUB - 1), skip_group_check=True)
                    mm.then_inc(g_mm, 1)

            def rows_w(c, w, ready, parity_col, done):
                pe.wait_ge(ready, c + 1)
                for q in range(SUB):
                    mm = pe.matmul(bank_of(c)[:, q * D:(q + 1) * D], ut[:, parity_col, q * P:(q + 1) * P], w[:, :],
                                   start=True, stop=True, skip_group_check=True)
                mm.then_inc(done, 1)

            x2w = [x2p[0][:, :], x2p[1][:, :]]
            panw = [pan[0][:, :], pan[1][:, :]]
            pe.wait_ge(x2lo_ok, NR)
            for J in range(NC):
                product(SCH, A_HALVES, x2w, J)
            with pe.Fori(1, C_CHUNKS) as k:
                n0 = k * (2 * NC) + A_HALVES
                for J in range(NC):
                    product(k + SCH, n0, x2w, J)
                    if J == 1:
                        add_neighbours(k - 1)
                    if J == 4:
                        rows_w(k - 1, w2s, v_ok, 0, w2_mm)
            n0 = A_HALVES + C_HALVES
            for J in range(NC):
                c = C_CHUNKS - 1 + J
                if c < NC:
                    add_neighbours(c)
                pe.wait_ge(x3lo_ok, J + 1)
                product(0, n0, panw, J)
                if c < NC:
                    rows_w(c, w2s, v_ok, 0, w2_mm)
            with pe.Fori(1, NC) as k:
                n0 = k * (2 * NC) + (A_HALVES + C_HALVES)
                for J in range(NC):
                    product(k, n0, panw, J)
                    if J == 1:
                        rows_w(k - 1, w3s, t_ok, 1, w3_mm)
            rows_w(NC - 1, w3s, t_ok, 1, w3_mm)

        @block.scalar
        def _(act):
            def hi_half(n, hf, src, buf):
                nc.scalar.activation(buf[:, hf, 0, :], src, ACT.Copy).then_inc(hi_made, 1)

            act.wait_ge(ln_ok, 1)
            for r in range(NR):
                nc.scalar.activation(h[:, r, :], xp[:, r, :], ACT.Relu, bias=shift[:, r:r + 1],
                                     scale=rstd[:, r:r + 1]).then_inc(h_ok, 1)

            def u_copy(c):
                act.wait_ge(split_used, 2 * COLBLK[c, NC - 1]["col"])
                if c >= 2:
                    act.wait_ge(zw_mm, c - 1)
                nc.scalar.copy(ut[:, c % 2, :], ps[:, c, :]).then_inc(u_ok, 1)

            def z_squares(c):
                act.wait_ge(z_ok, c + 1)
                if c:
                    act.wait_ge(sq_ok, SUB * c)
                for q in range(SUB):
                    nc.scalar.activation(x2s[:, q, :], zt[:, c % 2, q, :], ACT.Square,
                                         accum_out=sq[:, c * SUB + q:c * SUB + q + 1]).then_inc(sq_ok, 1)

            def z_hi(c):
                act.wait_ge(zt_mm, c + 1)
                act.wait_ge(row_done, N_ROW)
                nc.scalar.activation(pan[0][:, c * CH:(c + 1) * CH], ps[:, c, :], ACT.Copy).then_inc(zhi_ok, 1)

            for R in range(NC):
                act.wait_ge(xp_ok, SUB * (R + 1))
                if R >= 2:
                    act.wait_ge(split_used, 2 * COLBLK[R - 2, R - 2]["col"])
                nc.scalar.activation(xst[:, R % 2, 0, :], xp[:, R * SUB:(R + 1) * SUB, :].rearrange("p a f -> p (a f)"),
                                     ACT.Copy).then_inc(xhi_ok, 1)
                for r in range(R + 1):
                    ld = COLBLK[r, R]
                    act.wait_ge(blk_in[ld["slot"]], ld["landed"])
                    for hf in range(2):
                        n = 2 * (ld["col"] - 1) + hf
                        if n >= 2:
                            act.wait_ge(split_used, n - 1)
                        hi_half(n, hf, blk[:, ld["slot"], 2 * hf:2 * hf + 2, :].rearrange("p a c -> p (a c)"), split_a)
                    if R == NC - 1:
                        if r >= 1:
                            u_copy(r - 1)
                        if r >= 3:
                            z_squares(r - 3)
                            z_hi(r - 3)
            for c in range(NC - 3, NC):
                if c == NC - 3:
                    u_copy(NC - 1)
                z_squares(c)
                z_hi(c)
            act.wait_ge(ident_ok, 3)
            for g in range(4):
                act.wait_ge(sqp_mm, g + 1)
                nc.scalar.copy(negsq[0:3, 2 * g * CH:(2 * g + 2) * CH],
                               ps[0:3, 2 * g:2 * g + 2, :].rearrange("p a c -> p (a c)")).then_inc(negsq_ok, 1)

            def copy_scores(r, u):
                act.wait_ge(topi_ok, r - 1) if not (isinstance(r, int) and r < 2) else None
                for q in range(4):
                    act.wait_ge(zz_mm, r * 4 + (q + 1))
                    nc.scalar.copy(score[:, u % 2, 2 * q * CH:(2 * q + 2) * CH],
                                   ps[:, 4 + 2 * (q % 2):6 + 2 * (q % 2), :].rearrange("p a c -> p (a c)")
                                   ).then_inc(score_ok, 1)

            def row(t, r):
                return t[:, r, :] if isinstance(r, int) else t[:, ds(r, 1), :].rearrange("p a f -> p (a f)")

            def col(t, r):
                return t[:, r:r + 1] if isinstance(r, int) else t[:, ds(r, 1)]

            def panel(t, r):
                return t[:, r * P:(r + 1) * P] if isinstance(r, int) else t[:, ds(r * P, P)]

            def neighbours(r, u):
                act.wait_ge(dist_ok, 4 * r + 4)
                nc.scalar.activation(row(s4, r), dist[:, u, 3, :], ACT.Exp, scale=-0.5,
                                     accum_out=ssum[:, u:u + 1]).then_inc(s4_ok, 1)
                act.wait_ge(dis2_ok, r + 1)
                nc.scalar.activation(x2s[:, u, :], row(h, r), ACT.Copy, scale=col(dis2, r)).then_inc(x2_ok, 1)
                nc.scalar.activation(panel(x2p[0], r), row(h, r), ACT.Copy, scale=col(dis2, r)).then_inc(x2hi_ok, 1)
                act.wait_ge(x2_ok, r + 1)
                act.dma_start(x2d[r * P:(r + 1) * P, :] if isinstance(r, int) else x2d[ds(r * P, P), :],
                              x2s[:, u, :]).then_inc(x2_out, 16)

            act.wait_ge(sq_ok, NR)
            copy_scores(0, 0)
            with act.Fori(0, NR // GRP - 1) as it:
                act.wait_ge(x2_out, it * (16 * GRP))
                for u in range(GRP):
                    copy_scores(it * GRP + (u + 1), u + 1)
                    neighbours(it * GRP + u, u)
            act.wait_ge(x2_out, 16 * (NR - GRP))
            for u in range(GRP):
                r = NR - GRP + u
                if r + 1 < NR:
                    copy_scores(r + 1, u + 1)
                neighbours(r, u)

            def hi_block(n0, J, loads_before):
                ring_landed(act, J, loads_before)
                for hf in range(2):
                    act.wait_ge(split_used, n0 + (2 * J + hf - 1))
                    hi_half(0, hf, ring[:, J, 2 * hf:2 * hf + 2, :].rearrange("p a c -> p (a c)"), split_d)

            def bank_of(c):
                return ps[:, c, :] if isinstance(c, int) else ps[:, ds(c, 1), :].rearrange("p a c -> p (a c)")

            def v_copy(c):
                act.wait_ge(g_mm, c * SUB + SUB)
                act.wait_ge(w2_mm, c)
                nc.scalar.copy(ut[:, 0, :], bank_of(c)).then_inc(v_ok, 1)

            def x3(c):
                act.wait_ge(lnsc_ok, c * 5 + 5)
                act.wait_ge(x3lo_ok, c)
                for q in range(SUB):
                    nc.scalar.activation(x2s[:, q, :], row(h, c * SUB + q), ACT.Relu, bias=lnsc[:, 4, q:q + 1],
                                         scale=lnsc[:, 2, q:q + 1]).then_inc(x3_ok, 1)
                act.wait_ge(x3_ok, c * SUB + SUB)
                nc.scalar.activation(pan[0][:, c * CH:(c + 1) * CH] if isinstance(c, int) else pan[0][:, ds(c * CH, CH)],
                                     x2s[:, 0:SUB, :].rearrange("p a f -> p (a f)"), ACT.Copy).then_inc(x3hi_ok, 1)

            def t_copy(c):
                act.wait_ge(split_used, c * (2 * NC) + (A_HALVES + C_HALVES + 2 * NC))
                act.wait_ge(w3_mm, c)
                nc.scalar.copy(ut[:, 1, :], bank_of(c)).then_inc(t_ok, 1)

            act.wait_ge(topi_ok, NR)
            for J in range(NC):
                hi_block(A_HALVES, J, 0)
            with act.Fori(1, C_CHUNKS) as k:
                n0 = k * (2 * NC) + A_HALVES
                for J in range(NC):
                    hi_block(n0, J, k)
                    if J == 2:
                        v_copy(k - 1)
                    if J == 6:
                        x3(k - 1)
            n0 = A_HALVES + C_HALVES
            for J in range(NC):
                c = C_CHUNKS - 1 + J
                hi_block(n0, J, C_CHUNKS)
                if c < NC:
                    v_copy(c)
                    x3(c)
            with act.Fori(1, NC) as k:
                n0 = k * (2 * NC) + (A_HALVES + C_HALVES)
                for J in range(NC):
                    hi_block(n0, J, k + C_CHUNKS)
                    if J == 0:
                        t_copy(k - 1)
            t_copy(NC - 1)

            
        @block.vector
        def _(dve):
            def lo_half(hf, src, buf):
                nc.vector.tensor_tensor(buf[:, hf, 1, :], src, buf[:, hf, 0, :].bitcast(F32),
                                        ALU.subtract).then_inc(lo_made, 1)

            dve.wait_ge(x_in, 16)
            for r in range(NR):
                nc.vector.bn_stats(stats[:, r, :], xp[:, r, :]).then_inc(stats_ok, 1)
            dve.wait_ge(stats_ok, NR)
            for r in range(NR):
                nc.vector.bn_aggr(meanvar[:, r, :], stats[:, r, :]).then_inc(mv_ok, 1)

            def z_make(c):
                dve.wait_ge(zw_mm, c + 1)
                dve.wait_ge(b_in, 32)
                if c >= 2:
                    dve.wait_ge(zt_mm, c - 1)
                    dve.wait_ge(sq_ok, SUB * (c - 1))
                for q in range(SUB):
                    r = c * SUB + q
                    nc.vector.scalar_tensor_tensor(zt[:, c % 2, q, :], ps[:, c, q * D:(q + 1) * D], dis[:, r:r + 1],
                                                   b1s[:, :], ALU.mult, ALU.add).then_inc(zt_part, 1)
                dve.wait_ge(zt_part, SUB * (c + 1))
                zz = zt[:, c % 2, :, :].rearrange("p q f -> p (q f)")
                nc.vector.scalar_tensor_tensor(zz, zz, SLOPE, zz, ALU.mult, ALU.max).then_inc(z_ok, 1)

            def z_lo(c):
                dve.wait_ge(zhi_ok, c + 1)
                nc.vector.tensor_tensor(pan[1][:, c * CH:(c + 1) * CH], ps[:, c, :],
                                        pan[0][:, c * CH:(c + 1) * CH].bitcast(F32), ALU.subtract).then_inc(zlo_ok, 1)

            summed_at = 0
            for R in range(NC):
                for ld in SUMMED[R * NC:(R + 1) * NC]:
                    dve.wait_ge(blk_in[ld["slot"]], ld["landed"])
                    if R and summed_at == 0:
                        dve.wait_ge(deg_mm, R)
                    nc.vector.tensor_reduce(part[:, summed_at, :],
                                            blk[:, ld["slot"], :, :].rearrange("p s c -> p c s"),
                                            AX_X, ALU.add).then_inc(summed, 1)
                    summed_at = (summed_at + 1) % NC
                dve.wait_ge(deg_mm, R + 1)
                nc.vector.tensor_copy(deg[:, R * SUB:(R + 1) * SUB],
                                      ps[:, NC - 1, R * SUB:(R + 1) * SUB]).then_inc(deg_ok, 1)
                dve.wait_ge(dis_ok, R + 1)
                if R == 0:
                    dve.wait_ge(h_ok, NR)
                for q in range(SUB):
                    r = R * SUB + q
                    nc.vector.tensor_scalar(xp[:, r, :], h[:, r, :], dis[:, r:r + 1], None, ALU.mult).then_inc(xp_ok, 1)
                dve.wait_ge(xhi_ok, R + 1)
                nc.vector.tensor_tensor(xst[:, R % 2, 1, :], xp[:, R * SUB:(R + 1) * SUB, :].rearrange("p a f -> p (a f)"),
                                        xst[:, R % 2, 0, :].bitcast(F32), ALU.subtract).then_inc(xlo_ok, 1)
                for r in range(R + 1):
                    ld = COLBLK[r, R]
                    for hf in range(2):
                        n = 2 * (ld["col"] - 1) + hf
                        dve.wait_ge(hi_made, n + 1)
                        lo_half(hf, blk[:, ld["slot"], 2 * hf:2 * hf + 2, :].rearrange("p a c -> p (a c)"), split_a)
                    if R == NC - 1:
                        if r >= 2:
                            z_make(r - 2)
                        if r >= 4:
                            z_lo(r - 4)
            z_make(NC - 2)
            z_lo(NC - 4)
            z_make(NC - 1)
            for c in range(NC - 3, NC):
                z_lo(c)
            dve.wait_ge(sq_ok, NR)
            nc.vector.tensor_scalar(sqv[:, 0, :], sq[:, :], -0.5, None, ALU.mult).then_inc(sqv_ok, 1)
            dve.wait_ge(sqv_ok, 1)
            for g in range(3):
                nc.vector.tensor_copy(sqp[:, g, :], sqv[:, g, :]).then_inc(sqv_ok, 1)
                dve.wait_ge(sqv_ok, 2 * g + 2)
                if g < 2:
                    nc.vector.tensor_tensor(sqv[:, g + 1, :], sqv[:, g, :], sqp[:, g, :], ALU.subtract).then_inc(sqv_ok, 1)
                    dve.wait_ge(sqv_ok, 2 * g + 3)

            with dve.Fori(0, NR // GRP) as it:
                for u in range(GRP):
                    r = it * GRP + u
                    wait_apart(dve, score_ok, r * 4 + 4)
                    nc.vector.max(top[:, u, :], score[:, u % 2, :]).then_inc(top_ok, 1)
                    wait_apart(dve, top_ok, r + 1)
                    nc.vector.max_index(topi[:, u, :], top[:, u, :], score[:, u % 2, :]).then_inc(topi_ok, 1)

            def lo_block(n0, J):
                for hf in range(2):
                    dve.wait_ge(hi_made, n0 + (2 * J + hf + 1))
                    lo_half(hf, ring[:, J, 2 * hf:2 * hf + 2, :].rearrange("p a c -> p (a c)"), split_d)

            def weigh(c, q):
                r = c * SUB + q
                s4r = s4[:, r, :] if isinstance(r, int) else s4[:, ds(r, 1), :].rearrange("p a k -> p (a k)")
                dve.wait_ge(gathered[q], c * (16 * K) + 16 * K)
                nc.vector.tensor_scalar(xg[:, q, 0, :], xg[:, q, 0, :], s4r[:, 0:1], None, ALU.mult).then_inc(weighed, 1)
                for k in range(1, K):
                    dve.wait_ge(weighed, r * K + k)
                    nc.vector.scalar_tensor_tensor(xg[:, q, 0, :], xg[:, q, k, :], s4r[:, k:k + 1], xg[:, q, 0, :],
                                                   ALU.mult, ALU.add).then_inc(weighed, 1)

            def row(t, r):
                return t[:, r, :] if isinstance(r, int) else t[:, ds(r, 1), :].rearrange("p a f -> p (a f)")

            def col(t, r):
                return t[:, r:r + 1] if isinstance(r, int) else t[:, ds(r, 1)]

            def bank_of(c):
                return ps[:, c, :] if isinstance(c, int) else ps[:, ds(c, 1), :].rearrange("p a c -> p (a c)")

            def x1_rows(c):
                dve.wait_ge(w2_mm, c + 1)
                dve.wait_ge(lnsc_ok, c * 5)
                for q in range(SUB):
                    r = c * SUB + q
                    nc.vector.scalar_tensor_tensor(row(h, r), bank_of(c)[:, q * D:(q + 1) * D], col(dis2, r),
                                                   row(xb, r), ALU.mult, ALU.add).then_inc(x1_ok, 1)
                for q in range(SUB):
                    wait_apart(dve, x1_ok, c * SUB + (q + 1))
                    nc.vector.bn_stats(lnstat[:, q, :], row(h, c * SUB + q)).then_inc(lnst_ok, 1)
                for q in range(SUB):
                    wait_apart(dve, lnst_ok, c * SUB + (q + 1))
                    nc.vector.bn_aggr(lnmv[:, q, :], lnstat[:, q, :]).then_inc(lnmv_ok, 1)

            def x3_lo(c):
                dve.wait_ge(x3hi_ok, c + 1)
                hi = pan[0][:, c * CH:(c + 1) * CH] if isinstance(c, int) else pan[0][:, ds(c * CH, CH)]
                lo = pan[1][:, c * CH:(c + 1) * CH] if isinstance(c, int) else pan[1][:, ds(c * CH, CH)]
                nc.vector.tensor_tensor(lo, x2s[:, 0:SUB, :].rearrange("p a f -> p (a f)"), hi.bitcast(F32),
                                        ALU.subtract).then_inc(x3lo_ok, 1)

            def y_rows(c, par):
                dve.wait_ge(w3_mm, c + 1)
                for q in range(SUB):
                    r = c * SUB + q
                    nc.vector.scalar_tensor_tensor(row(h, r), bank_of(c)[:, q * D:(q + 1) * D], col(dis, r),
                                                   row(h, r), ALU.mult, ALU.add).then_inc(y_ok, 1)

            dve.wait_ge(xb_ok, 1)
            for J in range(NC):
                lo_block(A_HALVES, J)
                if J >= 4:
                    weigh(0, J - 4)
            with dve.Fori(1, C_CHUNKS) as k:
                n0 = k * (2 * NC) + A_HALVES
                for J in range(NC):
                    lo_block(n0, J)
                    if J == 4:
                        x1_rows(k - 1)
                    if J == 6:
                        x3_lo(k - 1)
                    if J >= 4:
                        weigh(k, J - 4)
            n0 = A_HALVES + C_HALVES
            for J in range(NC):
                c = C_CHUNKS - 1 + J
                lo_block(n0, J)
                if c < NC:
                    x1_rows(c)
                    x3_lo(c)
                    if c + 1 < NC:
                        for q in range(SUB):
                            weigh(c + 1, q)
            with dve.Fori(1, NC) as k:
                n0 = k * (2 * NC) + (A_HALVES + C_HALVES)
                for J in range(NC):
                    lo_block(n0, J)
                    if J == 2:
                        y_rows(k - 1, 0)
            y_rows(NC - 1, 0)

        @block.gpsimd
        def _(pool):
            nc.gpsimd.memset(ones[:, :], 1.0)
            nc.gpsimd.memset(ones16[:, :], 1.0)
            nc.gpsimd.memset(neghalf[:, :], -0.5)
            nc.gpsimd.memset(poshalf[:, :], 0.5).then_inc(consts, 1)
            nc.gpsimd.memset(ident[:, :], 0.0).then_inc(ident_z, 1)
            pool.wait_ge(ident_z, 1)
            nc.gpsimd.affine_select(out=ident[:, :], in_=ident[:, :], compare_op=ALU.not_equal, fill=1.0, base=0,
                                    pattern=[[-1, P]], channel_multiplier=1).then_inc(ident_ok, 1)
            pool.wait_ge(ident_ok, 1)
            nc.gpsimd.tensor_copy(ident16[:, :], ident[:, :]).then_inc(ident_ok, 1)
            nc.gpsimd.memset(negsq[:, :].bitcast(F32), 0.0).then_inc(ident_ok, 1)

            pool.wait_ge(mv_ok, NR)
            pool.wait_ge(consts, 1)
            nc.gpsimd.tensor_scalar(vareps[:, :], meanvar[:, :, 1], EPS, 1.0, ALU.add, ALU.mult).then_inc(ln_step, 1)
            nc.gpsimd.tensor_scalar(negmean[:, :], meanvar[:, :, 0], -1.0, 0.0, ALU.mult, ALU.add).then_inc(ln_step, 1)
            pool.wait_ge(ln_step, 2)
            nc.gpsimd.tensor_tensor(rstd[:, :], vareps[:, :], neghalf[:, :], ALU.pow).then_inc(ln_step, 1)
            pool.wait_ge(ln_step, 3)
            nc.gpsimd.tensor_tensor(shift[:, :], negmean[:, :], rstd[:, :], ALU.mult).then_inc(ln_ok, 1)

            for R in range(NC):
                pool.wait_ge(deg_ok, R + 1)
                c = slice(R * SUB, (R + 1) * SUB)
                nc.gpsimd.tensor_tensor(dis[:, c], deg[:, c], neghalf[:, c], ALU.pow).then_inc(dis_ok, 1)

            def stage_z(r, u):
                if not (isinstance(r, int) and r < 2):
                    pool.wait_ge(zz_mm, r * 4 - 4)
                for i in range(2):
                    src = pan[i][:, r * P:(r + 1) * P] if isinstance(r, int) else pan[i][:, ds(r * P, P)]
                    nc.gpsimd.tensor_copy(zslot[:, u % 2, i, :], src.bitcast(F32)).then_inc(zslot_ok, 1)

            def row(t, r):
                return t[:, r, :] if isinstance(r, int) else t[:, ds(r, 1), :].rearrange("p a f -> p (a f)")

            def col(t, r):
                return t[:, r:r + 1] if isinstance(r, int) else t[:, ds(r, 1)]

            def panel(t, r):
                return t[:, r * P:(r + 1) * P] if isinstance(r, int) else t[:, ds(r * P, P)]

            def distances(r, u):
                pool.wait_ge(topi_ok, r + 1)
                nc.gpsimd.tensor_copy(row(idx, r), topi[:, u, 0:K]).then_inc(idx_ok, 1)
                nc.gpsimd.tensor_scalar(dist[:, u, 0, :], top[:, u, 0:K], -2.0, 0.0, ALU.mult, ALU.add).then_inc(dist_ok, 1)
                pool.wait_ge(dist_ok, r * 4 + 1)
                nc.gpsimd.tensor_tensor(dist[:, u, 1, :], dist[:, u, 0, :], col(sq, r).broadcast_to([P, K]),
                                        ALU.add).then_inc(dist_ok, 1)
                wait_apart(pool, dist_ok, r * 4 + 2)
                nc.gpsimd.tensor_scalar(dist[:, u, 2, :], dist[:, u, 1, :], 0.0, 1e-10, ALU.max, ALU.add).then_inc(dist_ok, 1)
                pool.wait_ge(dist_ok, r * 4 + 3)
                nc.gpsimd.tensor_tensor(dist[:, u, 3, :], dist[:, u, 2, :], poshalf[:, :], ALU.pow).then_inc(dist_ok, 1)
                pool.wait_ge(s4_ok, r + 1)
                nc.gpsimd.tensor_tensor(deg2[:, u:u + 1], ssum[:, u:u + 1], col(deg, r), ALU.add).then_inc(deg2_ok, 1)
                pool.wait_ge(deg2_ok, r + 1)
                nc.gpsimd.tensor_tensor(col(dis2, r), deg2[:, u:u + 1], neghalf[:, 0:1], ALU.pow).then_inc(dis2_ok, 1)
                pool.wait_ge(x2hi_ok, r + 1)
                nc.gpsimd.tensor_tensor(panel(x2p[1], r), x2s[:, u, :], panel(x2p[0], r).bitcast(F32),
                                        ALU.subtract).then_inc(x2lo_ok, 1)

            pool.wait_ge(zlo_ok, NC)
            stage_z(0, 0)
            stage_z(1, 1)
            with pool.Fori(0, NR // GRP - 1) as it:
                for u in range(GRP):
                    stage_z(it * GRP + (u + 2), u)
                    distances(it * GRP + u, u)
            for u in range(GRP):
                r = NR - GRP + u
                if r + 2 < NR:
                    stage_z(r + 2, u)
                distances(r, u)

            pool.wait_ge(xb_in, 16)
            nc.gpsimd.tensor_tensor(xb[:, :, :], xb[:, :, :], b2s[:, :].rearrange("p (a f) -> p a f", a=1).broadcast_to([P, NR, D]),
                                    ALU.add).then_inc(xb_ok, 1)
            pool.wait_ge(x2_out, 16 * NR)

            def gather(c):
                for q in range(SUB):
                    r = c * SUB + q
                    if not (isinstance(c, int) and c == 0):
                        pool.wait_ge(g_mm, r - (SUB - 1))
                    nc.gpsimd.tensor_copy(idxs[:, q, :], row(idx, r)).then_inc(idxs_ok, 1)
                    wait_apart(pool, idxs_ok, r + 1)
                    for k in range(K):
                        nc.gpsimd.indirect_dma_start(
                            out=xg[:, q, k, :], out_offset=None, in_=x2d[:, :],
                            in_offset=bass.IndirectOffsetOnAxis(ap=idxs[:, q, k:k + 1], axis=0),
                        ).then_inc(gathered[q], 16)

            def ln_factors(c):
                pool.wait_ge(lnmv_ok, c * SUB + SUB)
                wait_apart(pool, x3_ok, c * SUB)
                disc = dis[:, c * SUB:(c + 1) * SUB] if isinstance(c, int) else dis[:, ds(c * SUB, SUB)]
                n = c * 5
                nc.gpsimd.tensor_scalar(lnsc[:, 0, :], lnmv[:, :, 1], EPS, 1.0, ALU.add, ALU.mult).then_inc(lnsc_ok, 1)
                nc.gpsimd.tensor_scalar(lnsc[:, 3, :], lnmv[:, :, 0], -1.0, 0.0, ALU.mult, ALU.add).then_inc(lnsc_ok, 1)
                pool.wait_ge(lnsc_ok, n + 2)
                nc.gpsimd.tensor_tensor(lnsc[:, 1, :], lnsc[:, 0, :], neghalf[:, 0:SUB], ALU.pow).then_inc(lnsc_ok, 1)
                pool.wait_ge(lnsc_ok, n + 3)
                nc.gpsimd.tensor_tensor(lnsc[:, 2, :], lnsc[:, 1, :], disc, ALU.mult).then_inc(lnsc_ok, 1)
                pool.wait_ge(lnsc_ok, n + 4)
                nc.gpsimd.tensor_tensor(lnsc[:, 4, :], lnsc[:, 3, :], lnsc[:, 2, :], ALU.mult).then_inc(lnsc_ok, 1)

            gather(0)
            with pool.Fori(0, NC - 1) as c:
                gather(c + 1)
                ln_factors(c)
            ln_factors(NC - 1)

            with pool.Fori(0, NC // 2) as it:
                for par in range(2):
                    c = it * 2 + par
                    pool.wait_ge(y_ok, c * SUB + SUB)
                    pool.dma_start(out[:, ds(c * SUB, SUB), :], h[:, ds(c * SUB, SUB), :]).then_inc(y_sent[par], 16)
                    

def kernel(x, adj, L0_gnn_W1, L0_gnn_b1, L0_gnn_W2, L0_gnn_b2, L1_gnn_weight):
    import numpy as np
    import concourse.bacc as bacc
    from concourse.bass_utils import run_bass_kernel_spmd as run

    xr = np.ascontiguousarray(np.asarray(x).reshape(NR, P, D).transpose(1, 0, 2))
    at = np.ascontiguousarray(np.asarray(adj).reshape(NC, CH, NC, SUB, P).transpose(0, 2, 4, 3, 1))
    arrays = {"in_x": xr, "in_at": at}
    for name, w in (("w1", L0_gnn_W1), ("b1", L0_gnn_b1), ("w2", L0_gnn_W2), ("b2", L0_gnn_b2), ("w3", L1_gnn_weight)):
        arrays["in_" + name] = np.ascontiguousarray(np.asarray(w))
    nc = bacc.Bacc("TRN2", target_bir_lowering=False, num_devices=1)
    ap = {n: nc.dram_tensor(n, a.shape, mybir.dt.from_np(a.dtype), kind="ExternalInput").ap() for n, a in arrays.items()}
    out = nc.dram_tensor("out_rows", (P, NR, D), F32, kind="ExternalOutput").ap()
    build(nc, ap["in_x"], ap["in_at"], ap["in_w1"], ap["in_b1"], ap["in_w2"], ap["in_b2"], ap["in_w3"], out)
    r = run(nc, [arrays], core_ids=[0])
    y = r.results[0]["out_rows"]
    return np.ascontiguousarray(y.transpose(1, 0, 2).reshape(N, D))
```

```python
from contextlib import ExitStack

import concourse.bass as bass
from concourse import mybir

F32 = mybir.dt.float32
F32R = mybir.dt.float32r
BF16 = mybir.dt.bfloat16
U32 = mybir.dt.uint32
ALU = mybir.AluOpType
ACT = mybir.ActivationFunctionType
AX_X = mybir.AxisListType.X
ds = bass.ds

P = 128
N = 4096
D = 128
CH = 512
NC = N // CH
SUB = CH // P
NR = N // P
HALF = SUB // 2 * CH
K = 4
EPS = 1e-5
SLOPE = 0.1

SLOTS = 13
RING = NC
SCH = 2
GRP = 8

KEPT = 2
DROPPED = {(r, J) for J in range(NC) for r in range(J) if J - r > KEPT}
PARTS = 4
DEPTH_A = 3
DEPTH_D = 4


def plan_phase_a():
    rows = [(R, J) for R in range(NC) for J in range(R)]
    cols = [(r, J) for J in range(NC) for r in range(J + 1)]
    loads, sums = [], 0
    for R in range(NC):
        order = [(R, J, True) for J in range(R, NC)]
        order += [(R, J, True) for J in range(R)]
        order += [(r, R, False) for r in range(R) if (r, R) in DROPPED]
        for r, J, first in order:
            sums += first
            ld = dict(r=r, J=J, reduced=sums if first else 0, row=0, col=0)
            if first and (r, J) in DROPPED:
                ld["key"] = (R, 0, J)
            elif J < r:
                ld["row"] = rows.index((r, J)) + 1
                ld["key"] = (r, 1, J)
            else:
                ld["col"] = cols.index((r, J)) + 1
                ld["key"] = (J, 2, r)
            loads.append(ld)
    owner, count = [None] * SLOTS, [0] * SLOTS
    for ld in loads:
        s = min(range(SLOTS), key=lambda i: (-1,) if owner[i] is None else owner[i]["key"])
        ld["slot"], ld["before"] = s, owner[s]
        owner[s] = ld
        count[s] += 1
        ld["landed"] = 16 * count[s]
    return loads


def adds(n):
    R, J = divmod(n, NC)
    return (NC - 1) * R + (J if J == 1 else max(J - 1, 0))


LOADS = plan_phase_a()
SUMMED = [ld for ld in LOADS if ld["reduced"]]
ROWBLK = {(ld["r"], ld["J"]): ld for ld in LOADS if ld["row"]}
COLBLK = {(ld["r"], ld["J"]): ld for ld in LOADS if ld["col"]}
N_ROW, N_COL = len(ROWBLK), len(COLBLK)
A_HALVES = 2 * N_COL
C_CHUNKS = NC - SCH
C_HALVES = 2 * NC * C_CHUNKS


def build(nc, x, at, w1, b1, w2, b2, w3, out):
    with ExitStack() as ctx:
        def sb(name, shape, dt=F32, stack=ctx):
            return stack.enter_context(nc.sbuf_tensor(name, shape, dt))

        def sem(name):
            return ctx.enter_context(nc.semaphore(name))

        h = sb("h", [P, NR, D])
        ut = sb("ut", [P, 2, CH])
        zt = sb("zt", [P, 2, SUB, D])
        negsq = sb("negsq", [P, N], BF16)
        x2s = sb("x2s", [P, GRP, D])
        zslot = sb("zslot", [P, 2, 2, P], F32R)
        w1s, w2s, w3s = (sb(n, [D, D]) for n in ("w1s", "w2s", "w3s"))
        b1s, b2s = sb("b1s", [P, D]), sb("b2s", [P, D])
        ident = sb("ident", [P, P])
        ident16 = sb("ident16", [P, P], BF16)
        ones16 = sb("ones16", [P, P], BF16)
        ones = sb("ones", [P, 1])
        neghalf = sb("neghalf", [P, NR])
        poshalf = sb("poshalf", [P, K])
        stats = sb("stats", [P, NR, 6])
        meanvar = sb("meanvar", [P, NR, 2])
        vareps = sb("vareps", [P, NR])
        rstd = sb("rstd", [P, NR])
        negmean = sb("negmean", [P, NR])
        shift = sb("shift", [P, NR])
        deg = sb("deg", [P, NR])
        dis = sb("dis", [P, NR])
        sq = sb("sq", [P, NR])
        sqv = sb("sqv", [P, 3, NR])
        sqp = sb("sqp", [P, 3, NR], BF16)
        dis2 = sb("dis2", [P, NR])
        s4 = sb("s4", [P, NR, K])
        idx = sb("idx", [P, NR, K], U32)
        top = sb("top", [P, GRP, 8])
        topi = sb("topi", [P, GRP, 8], U32)
        dist = sb("dist", [P, GRP, 4, K])
        ssum = sb("ssum", [P, GRP])
        deg2 = sb("deg2", [P, GRP])
        idxs = sb("idxs", [P, SUB, K], U32)
        lnstat = sb("lnstat", [P, SUB, 6])
        lnmv = sb("lnmv", [P, SUB, 2])
        lnsc = sb("lnsc", [P, 5, SUB])

        with ExitStack() as a:
            xp = sb("xp", [P, NR, D], F32, a)
            part = sb("part", [P, PARTS, CH], F32, a)
            xst = sb("xst", [P, 2, 2, CH], F32R, a)
            split_a = sb("split_a", [P, DEPTH_A, 2, HALF], F32R, a)
            blk = sb("blk", [P, SLOTS, SUB, CH], F32, a)
        pan = [sb("pan_hi", [P, N], F32R), sb("pan_lo", [P, N], F32R)]
        x2p = [sb("x2_hi", [P, N], F32R), sb("x2_lo", [P, N], F32R)]
        ring = sb("ring", [P, RING, SUB, CH])
        with ExitStack() as s:
            score = sb("score", [P, 2, N], F32, s)
        split_d = sb("split_d", [P, DEPTH_D, 2, HALF], F32R)
        xg = negsq[:, :].bitcast(F32).rearrange("p (q k f) -> p q k f", q=SUB, k=K)

        ps = ctx.enter_context(nc.psum_tensor("ps", [P, NC, CH], F32))
        x2d = nc.dram_tensor("x2_rows", (N, D), F32, kind="Internal").ap()

        x_in, w_in, b_in, xb_in = (sem(n) for n in ("x_in", "w_in", "b_in", "xb_in"))
        blk_in = [sem(f"blk_in{i}") for i in range(SLOTS)]
        ring_in = [sem(f"ring_in{i}") for i in range(RING)]
        consts, ident_z, ident_ok = sem("consts"), sem("ident_z"), sem("ident_ok")
        stats_ok, mv_ok, ln_step, ln_ok, h_ok = (sem(n) for n in ("stats_ok", "mv_ok", "ln_step", "ln_ok", "h_ok"))
        summed, added, deg_mm, deg_ok, dis_ok = (sem(n) for n in ("summed", "added", "deg_mm", "deg_ok", "dis_ok"))
        xp_ok, xhi_ok, xlo_ok = (sem(n) for n in ("xp_ok", "xhi_ok", "xlo_ok"))
        hi_made, lo_made, split_used = (sem(n) for n in ("hi_made", "lo_made", "split_used"))
        row_done, chunk1_done = sem("row_done"), sem("chunk1_done")
        u_ok, zw_mm, zt_part, z_ok, sq_ok = (sem(n) for n in ("u_ok", "zw_mm", "zt_part", "z_ok", "sq_ok"))
        zt_mm, zhi_ok, zlo_ok, sqv_ok, sqp_mm, negsq_ok = (
            sem(n) for n in ("zt_mm", "zhi_ok", "zlo_ok", "sqv_ok", "sqp_mm", "negsq_ok"))
        zslot_ok, zz_mm, score_ok, top_ok, topi_ok = (
            sem(n) for n in ("zslot_ok", "zz_mm", "score_ok", "top_ok", "topi_ok"))
        dist_ok, s4_ok, deg2_ok, dis2_ok, x2_ok, x2hi_ok, x2lo_ok, x2_out, x2_used, idx_ok = (
            sem(n) for n in ("dist_ok", "s4_ok", "deg2_ok", "dis2_ok", "x2_ok", "x2hi_ok", "x2lo_ok",
                             "x2_out", "x2_used", "idx_ok"))
        idxs_ok, gathered, weighed, g_mm = sem("idxs_ok"), [sem(f"gathered{q}") for q in range(SUB)], sem("weighed"), sem("g_mm")
        chunk2_done, v_ok, w2_mm, x1_ok, lnst_ok, lnmv_ok, lnsc_ok, x3_ok, x3hi_ok, x3lo_ok, xb_ok = (
            sem(n) for n in ("chunk2_done", "v_ok", "w2_mm", "x1_ok", "lnst_ok", "lnmv_ok", "lnsc_ok",
                             "x3_ok", "x3hi_ok", "x3lo_ok", "xb_ok"))
        chunk3_done, t_ok, w3_mm, y_ok = (sem(n) for n in ("chunk3_done", "t_ok", "w3_mm", "y_ok"))
        waited = sem("waited")
        y_sent = [sem("y_sent0"), sem("y_sent1")]

        def static(v):
            return isinstance(v, int)

        def wait_apart(eng, signal, value):
            eng.wait_ge(signal, value)
            eng.sem_inc(waited)

        block = ctx.enter_context(nc.Block())

        @block.sync
        def _(sp):
            sp.dma_start(xp[:, :, :], x[:, :, :]).then_inc(x_in, 16)

            for n, ld in enumerate(LOADS):
                old = ld["before"]
                if n == 2:
                    for dst, src in ((w1s, w1), (w2s, w2), (w3s, w3)):
                        sp.dma_start(dst[:, :], src[:, :]).then_inc(w_in, 16)
                    for dst, src in ((b1s, b1), (b2s, b2)):
                        sp.dma_start(dst[:, :], src.rearrange("(a f) -> a f", a=1).broadcast_to([P, D])).then_inc(b_in, 16)
                if old is not None:
                    if old["reduced"]:
                        sp.wait_ge(summed, old["reduced"])
                    if old["row"]:
                        sp.wait_ge(row_done, old["row"])
                    if old["col"]:
                        sp.wait_ge(lo_made, 2 * old["col"])
                sp.dma_start(blk[:, ld["slot"], :, :], at[ld["r"], ld["J"]]).then_inc(blk_in[ld["slot"]], 16)

            sp.wait_ge(lo_made, A_HALVES)
            sp.wait_ge(split_used, A_HALVES)

            def load_s(J, half):
                for c in range(SCH):
                    slot = SUB + 2 * half + c
                    sp.dma_start(ring[:, slot, :, :], at[c, J]).then_inc(ring_in[slot], 16)

            load_s(0, 0)
            load_s(1, 1)
            for J in range(SUB):
                sp.dma_start(ring[:, J, :, :], at[SCH, J]).then_inc(ring_in[J], 16)
            with sp.Fori(0, NC // 2 - 1) as it:
                for half in range(2):
                    sp.wait_ge(x2_used, it * GRP + SUB * (half + 1))
                    for c in range(SCH):
                        slot = SUB + 2 * half + c
                        sp.dma_start(ring[:, slot, :, :], at[c, ds(it * 2 + (2 + half), 1)].rearrange(
                            "a p s c -> (a p) s c")).then_inc(ring_in[slot], 16)
            for half in range(2):
                sp.wait_ge(x2_used, NR - SUB * (2 - half) + SUB)
                for c in range(SCH):
                    slot = SUB + 2 * half + c
                    sp.dma_start(ring[:, slot, :, :], at[SCH, slot]).then_inc(ring_in[slot], 16)
            with sp.Fori(1, C_CHUNKS) as k:
                for J in range(NC):
                    sp.wait_ge(lo_made, k * (2 * NC) + (A_HALVES - 2 * NC + 2 * J + 2))
                    sp.dma_start(ring[:, J, :, :], at[ds(k + SCH, 1), J].rearrange(
                        "a p s c -> (a p) s c")).then_inc(ring_in[J], 16)
            with sp.Fori(0, NC) as k:
                for J in range(NC):
                    sp.wait_ge(lo_made, k * (2 * NC) + (A_HALVES + C_HALVES - 2 * NC + 2 * J + 2))
                    sp.dma_start(ring[:, J, :, :], at[ds(k, 1), J].rearrange(
                        "a p s c -> (a p) s c")).then_inc(ring_in[J], 16)
            sp.wait_ge(y_sent[0], 16 * NC // 2)
            sp.wait_ge(y_sent[1], 16 * NC // 2)

        def ring_landed(eng, J, loads_before):
            base = NC // 2 if J >= SUB else 0
            eng.wait_ge(ring_in[J], loads_before * 16 + 16 * (base + 1))

        @block.tensor
        def _(pe):
            def split_half(bank, n, hf, w, wcol, first, last, slot=0):
                in_a = static(n) and n < A_HALVES
                part_of = split_a[:, n % DEPTH_A] if in_a else split_d[:, slot]
                for sub in range(SUB // 2):
                    c0 = wcol + (hf * (SUB // 2) + sub) * P
                    for g, (wi, ai) in enumerate(((0, 0), (1, 0), (0, 1))):
                        mm = pe.matmul(ps[:, bank, :] if static(bank) else
                                       ps[:, ds(bank, 1), :].rearrange("p a c -> p (a c)"),
                                       w[wi][:, c0:c0 + P],
                                       part_of[:, ai, sub * CH:(sub + 1) * CH],
                                       start=first and sub == 0 and g == 0,
                                       stop=last and sub == SUB // 2 - 1 and g == 2, skip_group_check=True)
                return mm

            def deg_sum(R):
                pe.wait_ge(added, adds(NC * (R + 1)))
                pe.wait_ge(consts, 1)
                for q in range(SUB):
                    mm = pe.matmul(ps[:, NC - 1, R * SUB + q:R * SUB + q + 1], ut[:, R % 2, q * P:(q + 1) * P],
                                   ones[:, :], start=True, stop=True, skip_group_check=True)
                mm.then_inc(deg_mm, 1)

            def row_block(R, J):
                ld = ROWBLK[R, J]
                pe.wait_ge(blk_in[ld["slot"]], ld["landed"])
                pe.wait_ge(xp_ok, SUB * (J + 1))
                for sub in range(SUB):
                    mm = pe.matmul(ps[:, R, :], xp[:, J * SUB + sub, :], blk[:, ld["slot"], sub, :],
                                   start=(J == 0 and sub == 0), stop=False, skip_group_check=True)
                mm.then_inc(row_done, 1)

            def col_block(r, J):
                ld = COLBLK[r, J]
                if r == 0:
                    pe.wait_ge(xlo_ok, J + 1)
                for hf in range(2):
                    n = 2 * (ld["col"] - 1) + hf
                    pe.wait_ge(lo_made, n + 1)
                    split_half(r, n, hf, [xst[:, J % 2, 0, :], xst[:, J % 2, 1, :]], 0,
                               J == 0 and hf == 0, J == NC - 1 and hf == 1).then_inc(split_used, 1)

            def z_rows(c):
                pe.wait_ge(u_ok, c + 1)
                pe.wait_ge(w_in, 48)
                for q in range(SUB):
                    mm = pe.matmul(ps[:, c, q * D:(q + 1) * D], ut[:, c % 2, q * P:(q + 1) * P], w1s[:, :],
                                   start=True, stop=True, skip_group_check=True)
                mm.then_inc(zw_mm, 1)

            def z_turn(c):
                pe.wait_ge(z_ok, c + 1)
                for q in range(SUB):
                    mm = pe.transpose(ps[:, c, q * P:(q + 1) * P], zt[:, c % 2, q, :], ident[:, :])
                mm.then_inc(zt_mm, 1)

            for R in range(NC):
                if R == NC - 1:
                    deg_sum(R)
                    pe.wait_ge(deg_ok, NC)
                for J in range(R):
                    if R < NC - 1 and J == max(R - 2, 0):
                        deg_sum(R)
                    row_block(R, J)
                if R == 0:
                    deg_sum(0)
                for r in range(R + 1):
                    col_block(r, R)
                    if R == NC - 1:
                        if r == 0:
                            pe.wait_ge(ident_ok, 1)
                        if r >= 1:
                            z_rows(r - 1)
                        if r >= 3:
                            z_turn(r - 3)
            z_turn(NC - 3)
            z_rows(NC - 1)
            z_turn(NC - 2)
            z_turn(NC - 1)
            pe.wait_ge(sqv_ok, 6)
            pe.wait_ge(ident_ok, 2)
            for r in range(NR):
                c = r // SUB
                if r % SUB == 0:
                    pe.wait_ge(zlo_ok, c + 1)
                mm = pe.matmul(ps[0:3, c, (r % SUB) * P:(r % SUB + 1) * P], sqp[:, :, r], ident16[:, :],
                               start=True, stop=True, skip_group_check=True)
                if r % (2 * SUB) == 2 * SUB - 1:
                    mm.then_inc(sqp_mm, 1)

            def zz(r, u):
                pe.wait_ge(zslot_ok, 2 * r + 2)
                for q in range(4):
                    unit = r * 4 + q
                    if not (static(r) and r == 0 and q < 2):
                        pe.wait_ge(score_ok, unit - 1)
                    for b in range(2):
                        bank = 4 + 2 * (q % 2) + b
                        cols = slice((2 * q + b) * CH, (2 * q + b + 1) * CH)
                        pe.matmul(ps[:, bank, :], ones16[:, :], negsq[:, cols], start=True, stop=False)
                        for g, (wi, mi) in enumerate(((0, 0), (1, 0), (0, 1))):
                            mm = pe.matmul(ps[:, bank, :], zslot[:, u % 2, wi, :], pan[mi][:, cols],
                                           start=False, stop=(g == 2))
                    mm.then_inc(zz_mm, 1)

            def product_s(r, u, it):
                if u % SUB == 0:
                    for c in range(SCH):
                        slot = SUB + 2 * (u // SUB) + c
                        pe.wait_ge(ring_in[slot], it * 16 + 16)
                pe.wait_ge(x2_ok, r + 1)
                for c in range(SCH):
                    mm = pe.matmul(ps[:, c, :], x2s[:, u, :], ring[:, SUB + 2 * (u // SUB) + c, u % SUB, :],
                                   start=static(r) and r == 0, stop=False, skip_group_check=True)
                mm.then_inc(x2_used, 1)

            pe.wait_ge(negsq_ok, 4)
            pe.wait_ge(consts, 1)
            zz(0, 0)
            zz(1, 1)
            for u in range(GRP):
                zz(u + 2, u)
                product_s(u, u, 0)
            with pe.Fori(1, NR // GRP - 1) as it:
                for u in range(GRP):
                    zz(it * GRP + (u + 2), u)
                    product_s(it * GRP + u, u, it)
            for u in range(GRP):
                r = NR - GRP + u
                if r + 2 < NR:
                    zz(r + 2, u)
                product_s(r, u, NR // GRP - 1)

            def product(bank, n0, panels, J):
                for hf in range(2):
                    pe.wait_ge(lo_made, n0 + (2 * J + hf + 1))
                    mm = split_half(bank, n0, hf, panels, J * CH, J == 0 and hf == 0, False, (2 * J + hf) % DEPTH_D)
                    mm.then_inc(split_used, 1)
                return mm

            def bank_of(c):
                return ps[:, c, :] if static(c) else ps[:, ds(c, 1), :].rearrange("p a c -> p (a c)")

            def add_neighbours(c):
                for q in range(SUB):
                    pe.wait_ge(weighed, c * (4 * SUB) + 4 * (q + 1))
                    mm = pe.matmul(bank_of(c)[:, q * P:(q + 1) * P], xg[:, q, 0, :], ident[:, :],
                                   start=False, stop=(q == SUB - 1), skip_group_check=True)
                    mm.then_inc(g_mm, 1)

            def rows_w(c, w, ready, parity_col, done):
                pe.wait_ge(ready, c + 1)
                for q in range(SUB):
                    mm = pe.matmul(bank_of(c)[:, q * D:(q + 1) * D], ut[:, parity_col, q * P:(q + 1) * P], w[:, :],
                                   start=True, stop=True, skip_group_check=True)
                mm.then_inc(done, 1)

            x2w = [x2p[0][:, :], x2p[1][:, :]]
            panw = [pan[0][:, :], pan[1][:, :]]
            pe.wait_ge(x2lo_ok, NR)
            for J in range(NC):
                product(SCH, A_HALVES, x2w, J)
            with pe.Fori(1, C_CHUNKS) as k:
                n0 = k * (2 * NC) + A_HALVES
                for J in range(NC):
                    product(k + SCH, n0, x2w, J)
                    if J == 1:
                        add_neighbours(k - 1)
                    if J == 4:
                        rows_w(k - 1, w2s, v_ok, 0, w2_mm)
            n0 = A_HALVES + C_HALVES
            for J in range(NC):
                c = C_CHUNKS - 1 + J
                if c < NC:
                    add_neighbours(c)
                pe.wait_ge(x3lo_ok, J + 1)
                product(0, n0, panw, J)
                if c < NC:
                    rows_w(c, w2s, v_ok, 0, w2_mm)
            with pe.Fori(1, NC) as k:
                n0 = k * (2 * NC) + (A_HALVES + C_HALVES)
                for J in range(NC):
                    product(k, n0, panw, J)
                    if J == 1:
                        rows_w(k - 1, w3s, t_ok, 1, w3_mm)
            rows_w(NC - 1, w3s, t_ok, 1, w3_mm)

        @block.scalar
        def _(act):
            def hi_half(src, buf, slot):
                nc.scalar.activation(buf[:, slot, 0, :], src, ACT.Copy).then_inc(hi_made, 1)

            act.wait_ge(ln_ok, 1)
            for r in range(NR):
                nc.scalar.activation(h[:, r, :], xp[:, r, :], ACT.Relu, bias=shift[:, r:r + 1],
                                     scale=rstd[:, r:r + 1]).then_inc(h_ok, 1)

            def u_copy(c):
                act.wait_ge(split_used, 2 * COLBLK[c, NC - 1]["col"])
                if c >= 2:
                    act.wait_ge(zw_mm, c - 1)
                nc.scalar.copy(ut[:, c % 2, :], ps[:, c, :]).then_inc(u_ok, 1)

            def z_squares(c):
                act.wait_ge(z_ok, c + 1)
                if c:
                    act.wait_ge(sq_ok, SUB * c)
                for q in range(SUB):
                    nc.scalar.activation(x2s[:, q, :], zt[:, c % 2, q, :], ACT.Square,
                                         accum_out=sq[:, c * SUB + q:c * SUB + q + 1]).then_inc(sq_ok, 1)

            def z_hi(c):
                act.wait_ge(zt_mm, c + 1)
                act.wait_ge(row_done, N_ROW)
                nc.scalar.activation(pan[0][:, c * CH:(c + 1) * CH], ps[:, c, :], ACT.Copy).then_inc(zhi_ok, 1)

            for R in range(NC):
                act.wait_ge(xp_ok, SUB * (R + 1))
                if R >= 2:
                    act.wait_ge(split_used, 2 * COLBLK[R - 2, R - 2]["col"])
                nc.scalar.activation(xst[:, R % 2, 0, :], xp[:, R * SUB:(R + 1) * SUB, :].rearrange("p a f -> p (a f)"),
                                     ACT.Copy).then_inc(xhi_ok, 1)
                for r in range(R + 1):
                    ld = COLBLK[r, R]
                    act.wait_ge(blk_in[ld["slot"]], ld["landed"])
                    for hf in range(2):
                        n = 2 * (ld["col"] - 1) + hf
                        if n >= DEPTH_A:
                            act.wait_ge(split_used, n - DEPTH_A + 1)
                        hi_half(blk[:, ld["slot"], 2 * hf:2 * hf + 2, :].rearrange("p a c -> p (a c)"), split_a,
                                n % DEPTH_A)
                    if R == NC - 1:
                        if r >= 1:
                            u_copy(r - 1)
                        if r >= 3:
                            z_squares(r - 3)
                            z_hi(r - 3)
            for c in range(NC - 3, NC):
                if c == NC - 3:
                    u_copy(NC - 1)
                z_squares(c)
                z_hi(c)
            act.wait_ge(ident_ok, 3)
            for g in range(4):
                act.wait_ge(sqp_mm, g + 1)
                nc.scalar.copy(negsq[0:3, 2 * g * CH:(2 * g + 2) * CH],
                               ps[0:3, 2 * g:2 * g + 2, :].rearrange("p a c -> p (a c)")).then_inc(negsq_ok, 1)

            def copy_scores(r, u):
                if not (static(r) and r < 2):
                    act.wait_ge(topi_ok, r - 1)
                for q in range(4):
                    act.wait_ge(zz_mm, r * 4 + (q + 1))
                    nc.scalar.copy(score[:, u % 2, 2 * q * CH:(2 * q + 2) * CH],
                                   ps[:, 4 + 2 * (q % 2):6 + 2 * (q % 2), :].rearrange("p a c -> p (a c)")
                                   ).then_inc(score_ok, 1)

            def row(t, r):
                return t[:, r, :] if static(r) else t[:, ds(r, 1), :].rearrange("p a f -> p (a f)")

            def col(t, r):
                return t[:, r:r + 1] if static(r) else t[:, ds(r, 1)]

            def panel(t, r):
                return t[:, r * P:(r + 1) * P] if static(r) else t[:, ds(r * P, P)]

            def neighbours(r, u):
                act.wait_ge(dist_ok, 4 * r + 4)
                nc.scalar.activation(row(s4, r), dist[:, u, 3, :], ACT.Exp, scale=-0.5,
                                     accum_out=ssum[:, u:u + 1]).then_inc(s4_ok, 1)
                act.wait_ge(dis2_ok, r + 1)
                nc.scalar.activation(x2s[:, u, :], row(h, r), ACT.Copy, scale=col(dis2, r)).then_inc(x2_ok, 1)
                nc.scalar.activation(panel(x2p[0], r), row(h, r), ACT.Copy, scale=col(dis2, r)).then_inc(x2hi_ok, 1)
                act.wait_ge(x2_ok, r + 1)
                act.dma_start(x2d[r * P:(r + 1) * P, :] if static(r) else x2d[ds(r * P, P), :],
                              x2s[:, u, :]).then_inc(x2_out, 16)

            act.wait_ge(sq_ok, NR)
            copy_scores(0, 0)

            def turn_s(it):
                if not (static(it) and it == 0):
                    act.wait_ge(x2_out, it * (16 * GRP))
                for u in range(GRP):
                    r = it * GRP + u
                    if not (static(it) and r + 1 == NR):
                        copy_scores(r + 1, u + 1)
                    neighbours(r, u)

            turn_s(0)
            with act.Fori(1, NR // GRP - 1) as it:
                turn_s(it)
            turn_s(NR // GRP - 1)

            def hi_block(n0, J, loads_before):
                ring_landed(act, J, loads_before)
                for hf in range(2):
                    act.wait_ge(split_used, n0 + (2 * J + hf - DEPTH_D + 1))
                    hi_half(ring[:, J, 2 * hf:2 * hf + 2, :].rearrange("p a c -> p (a c)"), split_d,
                            (2 * J + hf) % DEPTH_D)

            def bank_of(c):
                return ps[:, c, :] if static(c) else ps[:, ds(c, 1), :].rearrange("p a c -> p (a c)")

            def v_copy(c):
                act.wait_ge(g_mm, c * SUB + SUB)
                if not (static(c) and c == 0):
                    act.wait_ge(w2_mm, c)
                nc.scalar.copy(ut[:, 0, :], bank_of(c)).then_inc(v_ok, 1)

            def x3(c):
                act.wait_ge(lnsc_ok, c * 5 + 5)
                if not (static(c) and c == 0):
                    act.wait_ge(x3lo_ok, c)
                for q in range(SUB):
                    nc.scalar.activation(x2s[:, q, :], row(h, c * SUB + q), ACT.Relu, bias=lnsc[:, 4, q:q + 1],
                                         scale=lnsc[:, 2, q:q + 1]).then_inc(x3_ok, 1)
                act.wait_ge(x3_ok, c * SUB + SUB)
                nc.scalar.activation(pan[0][:, c * CH:(c + 1) * CH] if static(c) else pan[0][:, ds(c * CH, CH)],
                                     x2s[:, 0:SUB, :].rearrange("p a f -> p (a f)"), ACT.Copy).then_inc(x3hi_ok, 1)

            def t_copy(c):
                act.wait_ge(split_used, c * (2 * NC) + (A_HALVES + C_HALVES + 2 * NC))
                if not (static(c) and c == 0):
                    act.wait_ge(w3_mm, c)
                nc.scalar.copy(ut[:, 1, :], bank_of(c)).then_inc(t_ok, 1)

            act.wait_ge(topi_ok, NR)
            for J in range(NC):
                hi_block(A_HALVES, J, 0)

            def turn_c(k):
                n0 = k * (2 * NC) + A_HALVES
                for J in range(NC):
                    hi_block(n0, J, k)
                    if J == 2:
                        v_copy(k - 1)
                    if J == 6:
                        x3(k - 1)

            turn_c(1)
            with act.Fori(2, C_CHUNKS) as k:
                turn_c(k)
            n0 = A_HALVES + C_HALVES
            for J in range(NC):
                c = C_CHUNKS - 1 + J
                hi_block(n0, J, C_CHUNKS)
                if c < NC:
                    v_copy(c)
                    x3(c)

            def turn_d(k):
                n0 = k * (2 * NC) + (A_HALVES + C_HALVES)
                for J in range(NC):
                    hi_block(n0, J, k + C_CHUNKS)
                    if J == 0:
                        t_copy(k - 1)

            turn_d(1)
            with act.Fori(2, NC) as k:
                turn_d(k)
            t_copy(NC - 1)

            
        @block.vector
        def _(dve):
            def lo_half(src, buf, slot):
                nc.vector.tensor_tensor(buf[:, slot, 1, :], src, buf[:, slot, 0, :].bitcast(F32),
                                        ALU.subtract).then_inc(lo_made, 1)

            dve.wait_ge(x_in, 16)
            for r in range(NR):
                nc.vector.bn_stats(stats[:, r, :], xp[:, r, :]).then_inc(stats_ok, 1)
            dve.wait_ge(stats_ok, NR)
            for r in range(NR):
                nc.vector.bn_aggr(meanvar[:, r, :], stats[:, r, :]).then_inc(mv_ok, 1)

            def z_make(c):
                dve.wait_ge(zw_mm, c + 1)
                dve.wait_ge(b_in, 32)
                if c >= 2:
                    dve.wait_ge(zt_mm, c - 1)
                    dve.wait_ge(sq_ok, SUB * (c - 1))
                for q in range(SUB):
                    r = c * SUB + q
                    nc.vector.scalar_tensor_tensor(zt[:, c % 2, q, :], ps[:, c, q * D:(q + 1) * D], dis[:, r:r + 1],
                                                   b1s[:, :], ALU.mult, ALU.add).then_inc(zt_part, 1)
                dve.wait_ge(zt_part, SUB * (c + 1))
                zz = zt[:, c % 2, :, :].rearrange("p q f -> p (q f)")
                nc.vector.scalar_tensor_tensor(zz, zz, SLOPE, zz, ALU.mult, ALU.max).then_inc(z_ok, 1)

            def z_lo(c):
                dve.wait_ge(zhi_ok, c + 1)
                nc.vector.tensor_tensor(pan[1][:, c * CH:(c + 1) * CH], ps[:, c, :],
                                        pan[0][:, c * CH:(c + 1) * CH].bitcast(F32), ALU.subtract).then_inc(zlo_ok, 1)

            def degree_sum(n):
                ld = SUMMED[n]
                dve.wait_ge(blk_in[ld["slot"]], ld["landed"])
                if n >= PARTS:
                    dve.wait_ge(added, adds(n - PARTS + 1))
                nc.vector.tensor_reduce(part[:, n % PARTS, :], blk[:, ld["slot"], :, :].rearrange("p s c -> p c s"),
                                        AX_X, ALU.add).then_inc(summed, 1)

            n_sum = 0
            for R in range(NC):
                while n_sum < NC * (R + 1):
                    degree_sum(n_sum)
                    n_sum += 1
                dve.wait_ge(deg_mm, R + 1)
                nc.vector.tensor_copy(deg[:, R * SUB:(R + 1) * SUB],
                                      ps[:, NC - 1, R * SUB:(R + 1) * SUB]).then_inc(deg_ok, 1)
                dve.wait_ge(dis_ok, R + 1)
                if R == 0:
                    dve.wait_ge(h_ok, NR)
                for q in range(SUB):
                    r = R * SUB + q
                    nc.vector.tensor_scalar(xp[:, r, :], h[:, r, :], dis[:, r:r + 1], None, ALU.mult).then_inc(xp_ok, 1)
                dve.wait_ge(xhi_ok, R + 1)
                nc.vector.tensor_tensor(xst[:, R % 2, 1, :], xp[:, R * SUB:(R + 1) * SUB, :].rearrange("p a f -> p (a f)"),
                                        xst[:, R % 2, 0, :].bitcast(F32), ALU.subtract).then_inc(xlo_ok, 1)
                for r in range(R + 1):
                    ld = COLBLK[r, R]
                    for hf in range(2):
                        n = 2 * (ld["col"] - 1) + hf
                        dve.wait_ge(hi_made, n + 1)
                        lo_half(blk[:, ld["slot"], 2 * hf:2 * hf + 2, :].rearrange("p a c -> p (a c)"), split_a,
                                n % DEPTH_A)
                    while R < NC - 1 and n_sum < NC * (R + 1) + (r + 1) * NC // (R + 1):
                        degree_sum(n_sum)
                        n_sum += 1
                    if R == NC - 1:
                        if r >= 2:
                            z_make(r - 2)
                        if r >= 4:
                            z_lo(r - 4)
            z_make(NC - 2)
            z_lo(NC - 4)
            z_make(NC - 1)
            for c in range(NC - 3, NC):
                z_lo(c)
            dve.wait_ge(sq_ok, NR)
            nc.vector.tensor_scalar(sqv[:, 0, :], sq[:, :], -0.5, None, ALU.mult).then_inc(sqv_ok, 1)
            dve.wait_ge(sqv_ok, 1)
            for g in range(3):
                nc.vector.tensor_copy(sqp[:, g, :], sqv[:, g, :]).then_inc(sqv_ok, 1)
                dve.wait_ge(sqv_ok, 2 * g + 2)
                if g < 2:
                    nc.vector.tensor_tensor(sqv[:, g + 1, :], sqv[:, g, :], sqp[:, g, :], ALU.subtract).then_inc(sqv_ok, 1)
                    dve.wait_ge(sqv_ok, 2 * g + 3)

            with dve.Fori(0, NR // GRP) as it:
                for u in range(GRP):
                    r = it * GRP + u
                    wait_apart(dve, score_ok, r * 4 + 4)
                    nc.vector.max(top[:, u, :], score[:, u % 2, :]).then_inc(top_ok, 1)
                    wait_apart(dve, top_ok, r + 1)
                    nc.vector.max_index(topi[:, u, :], top[:, u, :], score[:, u % 2, :]).then_inc(topi_ok, 1)

            def lo_block(n0, J):
                for hf in range(2):
                    dve.wait_ge(hi_made, n0 + (2 * J + hf + 1))
                    lo_half(ring[:, J, 2 * hf:2 * hf + 2, :].rearrange("p a c -> p (a c)"), split_d,
                            (2 * J + hf) % DEPTH_D)

            def weigh(c, q):
                r = c * SUB + q
                s4r = s4[:, r, :] if static(r) else s4[:, ds(r, 1), :].rearrange("p a k -> p (a k)")
                dve.wait_ge(gathered[q], c * (16 * K) + 16 * K)
                nc.vector.tensor_scalar(xg[:, q, 0, :], xg[:, q, 0, :], s4r[:, 0:1], None, ALU.mult).then_inc(weighed, 1)
                for k in range(1, K):
                    dve.wait_ge(weighed, r * K + k)
                    nc.vector.scalar_tensor_tensor(xg[:, q, 0, :], xg[:, q, k, :], s4r[:, k:k + 1], xg[:, q, 0, :],
                                                   ALU.mult, ALU.add).then_inc(weighed, 1)

            def row(t, r):
                return t[:, r, :] if static(r) else t[:, ds(r, 1), :].rearrange("p a f -> p (a f)")

            def col(t, r):
                return t[:, r:r + 1] if static(r) else t[:, ds(r, 1)]

            def bank_of(c):
                return ps[:, c, :] if static(c) else ps[:, ds(c, 1), :].rearrange("p a c -> p (a c)")

            def x1_rows(c):
                dve.wait_ge(w2_mm, c + 1)
                dve.wait_ge(xb_ok, c + 1)
                if not (static(c) and c == 0):
                    dve.wait_ge(lnsc_ok, c * 5)
                for q in range(SUB):
                    r = c * SUB + q
                    nc.vector.scalar_tensor_tensor(row(h, r), bank_of(c)[:, q * D:(q + 1) * D], col(dis2, r),
                                                   zt[:, 1, q, :], ALU.mult, ALU.add).then_inc(x1_ok, 1)
                for q in range(SUB):
                    wait_apart(dve, x1_ok, c * SUB + (q + 1))
                    nc.vector.bn_stats(lnstat[:, q, :], row(h, c * SUB + q)).then_inc(lnst_ok, 1)
                for q in range(SUB):
                    wait_apart(dve, lnst_ok, c * SUB + (q + 1))
                    nc.vector.bn_aggr(lnmv[:, q, :], lnstat[:, q, :]).then_inc(lnmv_ok, 1)

            def x3_lo(c):
                dve.wait_ge(x3hi_ok, c + 1)
                hi = pan[0][:, c * CH:(c + 1) * CH] if static(c) else pan[0][:, ds(c * CH, CH)]
                lo = pan[1][:, c * CH:(c + 1) * CH] if static(c) else pan[1][:, ds(c * CH, CH)]
                nc.vector.tensor_tensor(lo, x2s[:, 0:SUB, :].rearrange("p a f -> p (a f)"), hi.bitcast(F32),
                                        ALU.subtract).then_inc(x3lo_ok, 1)

            def y_rows(c, par):
                dve.wait_ge(w3_mm, c + 1)
                for q in range(SUB):
                    r = c * SUB + q
                    nc.vector.scalar_tensor_tensor(row(h, r), bank_of(c)[:, q * D:(q + 1) * D], col(dis, r),
                                                   row(h, r), ALU.mult, ALU.add).then_inc(y_ok, 1)

            dve.wait_ge(split_used, A_HALVES)
            for J in range(NC):
                lo_block(A_HALVES, J)
                if J >= 4:
                    weigh(0, J - 4)

            def turn_c(k):
                n0 = k * (2 * NC) + A_HALVES
                for J in range(NC):
                    lo_block(n0, J)
                    if J == 4:
                        x1_rows(k - 1)
                    if J == 6:
                        x3_lo(k - 1)
                    if J >= 4:
                        weigh(k, J - 4)

            turn_c(1)
            with dve.Fori(2, C_CHUNKS) as k:
                turn_c(k)
            n0 = A_HALVES + C_HALVES
            for J in range(NC):
                c = C_CHUNKS - 1 + J
                lo_block(n0, J)
                if c < NC:
                    x1_rows(c)
                    x3_lo(c)
                    if c + 1 < NC:
                        for q in range(SUB):
                            weigh(c + 1, q)
            with dve.Fori(1, NC) as k:
                n0 = k * (2 * NC) + (A_HALVES + C_HALVES)
                for J in range(NC):
                    lo_block(n0, J)
                    if J == 2:
                        y_rows(k - 1, 0)
            y_rows(NC - 1, 0)

        @block.gpsimd
        def _(pool):
            nc.gpsimd.memset(ones[:, :], 1.0)
            nc.gpsimd.memset(ones16[:, :], 1.0)
            nc.gpsimd.memset(neghalf[:, :], -0.5)
            nc.gpsimd.memset(poshalf[:, :], 0.5).then_inc(consts, 1)
            nc.gpsimd.memset(ident[:, :], 0.0).then_inc(ident_z, 1)
            pool.wait_ge(ident_z, 1)
            nc.gpsimd.affine_select(out=ident[:, :], in_=ident[:, :], compare_op=ALU.not_equal, fill=1.0, base=0,
                                    pattern=[[-1, P]], channel_multiplier=1).then_inc(ident_ok, 1)
            pool.wait_ge(ident_ok, 1)
            nc.gpsimd.tensor_copy(ident16[:, :], ident[:, :]).then_inc(ident_ok, 1)
            nc.gpsimd.memset(negsq[:, :].bitcast(F32), 0.0).then_inc(ident_ok, 1)

            pool.wait_ge(mv_ok, NR)
            pool.wait_ge(consts, 1)
            nc.gpsimd.tensor_scalar(vareps[:, :], meanvar[:, :, 1], EPS, 1.0, ALU.add, ALU.mult).then_inc(ln_step, 1)
            nc.gpsimd.tensor_scalar(negmean[:, :], meanvar[:, :, 0], -1.0, 0.0, ALU.mult, ALU.add).then_inc(ln_step, 1)
            pool.wait_ge(ln_step, 2)
            nc.gpsimd.tensor_tensor(rstd[:, :], vareps[:, :], neghalf[:, :], ALU.pow).then_inc(ln_step, 1)
            pool.wait_ge(ln_step, 3)
            nc.gpsimd.tensor_tensor(shift[:, :], negmean[:, :], rstd[:, :], ALU.mult).then_inc(ln_ok, 1)

            for R in range(NC):
                for J in range(1, NC):
                    n = R * NC + J
                    pool.wait_ge(summed, n + 1)
                    if J == 1 and R >= 2:
                        pool.wait_ge(deg_mm, R - 1)
                    if J > 1:
                        pool.wait_ge(added, adds(n))
                    nc.gpsimd.tensor_tensor(ut[:, R % 2, :], part[:, 0, :] if J == 1 else ut[:, R % 2, :],
                                            part[:, n % PARTS, :], ALU.add).then_inc(added, 1)
                pool.wait_ge(deg_ok, R + 1)
                c = slice(R * SUB, (R + 1) * SUB)
                nc.gpsimd.tensor_tensor(dis[:, c], deg[:, c], neghalf[:, c], ALU.pow).then_inc(dis_ok, 1)

            def stage_z(r, u):
                if not (static(r) and r < 2):
                    pool.wait_ge(zz_mm, r * 4 - 4)
                for i in range(2):
                    src = pan[i][:, r * P:(r + 1) * P] if static(r) else pan[i][:, ds(r * P, P)]
                    nc.gpsimd.tensor_copy(zslot[:, u % 2, i, :], src.bitcast(F32)).then_inc(zslot_ok, 1)

            def row(t, r):
                return t[:, r, :] if static(r) else t[:, ds(r, 1), :].rearrange("p a f -> p (a f)")

            def col(t, r):
                return t[:, r:r + 1] if static(r) else t[:, ds(r, 1)]

            def panel(t, r):
                return t[:, r * P:(r + 1) * P] if static(r) else t[:, ds(r * P, P)]

            def distances(r, u):
                pool.wait_ge(topi_ok, r + 1)
                nc.gpsimd.tensor_copy(row(idx, r), topi[:, u, 0:K]).then_inc(idx_ok, 1)
                nc.gpsimd.tensor_scalar(dist[:, u, 0, :], top[:, u, 0:K], -2.0, 0.0, ALU.mult, ALU.add).then_inc(dist_ok, 1)
                pool.wait_ge(dist_ok, r * 4 + 1)
                nc.gpsimd.tensor_tensor(dist[:, u, 1, :], dist[:, u, 0, :], col(sq, r).broadcast_to([P, K]),
                                        ALU.add).then_inc(dist_ok, 1)
                wait_apart(pool, dist_ok, r * 4 + 2)
                nc.gpsimd.tensor_scalar(dist[:, u, 2, :], dist[:, u, 1, :], 0.0, 1e-10, ALU.max, ALU.add).then_inc(dist_ok, 1)
                pool.wait_ge(dist_ok, r * 4 + 3)
                nc.gpsimd.tensor_tensor(dist[:, u, 3, :], dist[:, u, 2, :], poshalf[:, :], ALU.pow).then_inc(dist_ok, 1)
                pool.wait_ge(s4_ok, r + 1)
                nc.gpsimd.tensor_tensor(deg2[:, u:u + 1], ssum[:, u:u + 1], col(deg, r), ALU.add).then_inc(deg2_ok, 1)
                pool.wait_ge(deg2_ok, r + 1)
                nc.gpsimd.tensor_tensor(col(dis2, r), deg2[:, u:u + 1], neghalf[:, 0:1], ALU.pow).then_inc(dis2_ok, 1)
                pool.wait_ge(x2hi_ok, r + 1)
                nc.gpsimd.tensor_tensor(panel(x2p[1], r), x2s[:, u, :], panel(x2p[0], r).bitcast(F32),
                                        ALU.subtract).then_inc(x2lo_ok, 1)

            pool.wait_ge(zlo_ok, NC)
            stage_z(0, 0)
            stage_z(1, 1)
            with pool.Fori(0, NR // GRP - 1) as it:
                for u in range(GRP):
                    stage_z(it * GRP + (u + 2), u)
                    distances(it * GRP + u, u)
            for u in range(GRP):
                r = NR - GRP + u
                if r + 2 < NR:
                    stage_z(r + 2, u)
                distances(r, u)

            def x_rows_in(c):
                if not (static(c) and c == 0):
                    wait_apart(pool, xb_ok, c)
                src = x[:, c * SUB:(c + 1) * SUB, :] if static(c) else x[:, ds(c * SUB, SUB), :]
                pool.dma_start(zt[:, 0, :, :], src).then_inc(xb_in, 16)

            def add_b2(c):
                pool.wait_ge(xb_in, c * 16 + 16)
                if not (static(c) and c == 0):
                    pool.wait_ge(x1_ok, c * SUB)
                nc.gpsimd.tensor_tensor(zt[:, 1, :, :], zt[:, 0, :, :],
                                        b2s[:, :].rearrange("p (a f) -> p a f", a=1).broadcast_to([P, SUB, D]),
                                        ALU.add).then_inc(xb_ok, 1)

            x_rows_in(0)
            pool.wait_ge(x2_out, 16 * NR)

            def gather(c):
                for q in range(SUB):
                    r = c * SUB + q
                    if not (static(c) and c == 0):
                        pool.wait_ge(g_mm, r - (SUB - 1))
                    nc.gpsimd.tensor_copy(idxs[:, q, :], row(idx, r)).then_inc(idxs_ok, 1)
                    wait_apart(pool, idxs_ok, r + 1)
                    for k in range(K):
                        nc.gpsimd.indirect_dma_start(
                            out=xg[:, q, k, :], out_offset=None, in_=x2d[:, :],
                            in_offset=bass.IndirectOffsetOnAxis(ap=idxs[:, q, k:k + 1], axis=0),
                        ).then_inc(gathered[q], 16)

            def ln_factors(c):
                wait_apart(pool, lnmv_ok, c * SUB + SUB)
                if not (static(c) and c == 0):
                    wait_apart(pool, x3_ok, c * SUB)
                disc = dis[:, c * SUB:(c + 1) * SUB] if static(c) else dis[:, ds(c * SUB, SUB)]
                n = c * 5
                nc.gpsimd.tensor_scalar(lnsc[:, 0, :], lnmv[:, :, 1], EPS, 1.0, ALU.add, ALU.mult).then_inc(lnsc_ok, 1)
                nc.gpsimd.tensor_scalar(lnsc[:, 3, :], lnmv[:, :, 0], -1.0, 0.0, ALU.mult, ALU.add).then_inc(lnsc_ok, 1)
                pool.wait_ge(lnsc_ok, n + 2)
                nc.gpsimd.tensor_tensor(lnsc[:, 1, :], lnsc[:, 0, :], neghalf[:, 0:SUB], ALU.pow).then_inc(lnsc_ok, 1)
                pool.wait_ge(lnsc_ok, n + 3)
                nc.gpsimd.tensor_tensor(lnsc[:, 2, :], lnsc[:, 1, :], disc, ALU.mult).then_inc(lnsc_ok, 1)
                pool.wait_ge(lnsc_ok, n + 4)
                nc.gpsimd.tensor_tensor(lnsc[:, 4, :], lnsc[:, 3, :], lnsc[:, 2, :], ALU.mult).then_inc(lnsc_ok, 1)

            gather(0)

            def turn_c(c):
                add_b2(c)
                x_rows_in(c + 1)
                gather(c + 1)
                ln_factors(c)

            turn_c(0)
            with pool.Fori(1, NC - 1) as c:
                turn_c(c)
            add_b2(NC - 1)
            ln_factors(NC - 1)

            with pool.Fori(0, NC // 2) as it:
                for par in range(2):
                    c = it * 2 + par
                    pool.wait_ge(y_ok, c * SUB + SUB)
                    pool.dma_start(out[:, ds(c * SUB, SUB), :], h[:, ds(c * SUB, SUB), :]).then_inc(y_sent[par], 16)
                    

def kernel(x, adj, L0_gnn_W1, L0_gnn_b1, L0_gnn_W2, L0_gnn_b2, L1_gnn_weight):
    import numpy as np
    import concourse.bacc as bacc
    from concourse.bass_utils import run_bass_kernel_spmd as run

    xr = np.ascontiguousarray(np.asarray(x).reshape(NR, P, D).transpose(1, 0, 2))
    at = np.ascontiguousarray(np.asarray(adj).reshape(NC, CH, NC, SUB, P).transpose(0, 2, 4, 3, 1))
    arrays = {"in_x": xr, "in_at": at}
    for name, w in (("w1", L0_gnn_W1), ("b1", L0_gnn_b1), ("w2", L0_gnn_W2), ("b2", L0_gnn_b2), ("w3", L1_gnn_weight)):
        arrays["in_" + name] = np.ascontiguousarray(np.asarray(w))
    nc = bacc.Bacc("TRN2", target_bir_lowering=False, num_devices=1)
    ap = {n: nc.dram_tensor(n, a.shape, mybir.dt.from_np(a.dtype), kind="ExternalInput").ap() for n, a in arrays.items()}
    out = nc.dram_tensor("out_rows", (P, NR, D), F32, kind="ExternalOutput").ap()
    build(nc, ap["in_x"], ap["in_at"], ap["in_w1"], ap["in_b1"], ap["in_w2"], ap["in_b2"], ap["in_w3"], out)
    r = run(nc, [arrays], core_ids=[0])
    y = r.results[0]["out_rows"]
    return np.ascontiguousarray(y.transpose(1, 0, 2).reshape(N, D))
```

```python
from contextlib import ExitStack

import concourse.bass as bass
from concourse import mybir

F32 = mybir.dt.float32
F32R = mybir.dt.float32r
BF16 = mybir.dt.bfloat16
U32 = mybir.dt.uint32
ALU = mybir.AluOpType
ACT = mybir.ActivationFunctionType
AX_X = mybir.AxisListType.X
ds = bass.ds

P = 128
N = 4096
D = 128
CH = 512
NC = N // CH
SUB = CH // P
NR = N // P
HALF = SUB // 2 * CH
K = 4
EPS = 1e-5
SLOPE = 0.1

SLOTS = 13
RING = NC
SPARE = 4
SCH = 2
GRP = 8

KEPT = 3
DROPPED = {(r, J) for J in range(NC) for r in range(J) if J - r > KEPT} | {(2, 5)}
PARTS = 4
DEPTH_A = 3
DEPTH_D = 4


Z = dict(u=2, rows=2, make=3, turn=3, squares=4, hi=5, lo=5)
NEG = dict(parts=5, spread=6, copy=7)
FIRST_SCORES = (11, 12, 14, 15)
FIRST_COPIES = (12, 13, 14, 15)
Z_TURNS = NC + 8


def stage(R):
    if R == NC:
        return [(None, [r]) for r in range(NC)]
    early = max(R - 1, 0)
    turns = [(J, list(range(-(-J * early // NC), -(-(J + 1) * early // NC)))) for J in range(NC)]
    return turns + ([(None, [R - 1])] if R else [])


def plan_phase_a():
    rows = [(R, J) for R in range(NC) for J in range(R)]
    cols = [(r, J) for J in range(NC) for r in range(J + 1)]
    freed = {}
    for R in range(NC + 1):
        for i, (_, rs) in enumerate(stage(R)):
            freed.update({(r, R - 1): (R, i) for r in rs})
    loads, sums = [], 0
    for R in range(NC):
        order = [(R, J, True) for J in range(NC)]
        order += [(r, R, False) for r in range(R) if (r, R) in DROPPED]
        for i, (r, J, first) in enumerate(order):
            sums += first
            ld = dict(r=r, J=J, reduced=sums if first else 0, row=0, col=0)
            if first and (r, J) in DROPPED:
                ld["key"] = (R, i)
            elif J < r:
                ld["row"] = rows.index((r, J)) + 1
                ld["key"] = (R, i + 1)
            else:
                ld["col"] = cols.index((r, J)) + 1
                ld["key"] = freed[r, J]
            loads.append(ld)
    owner, count = [None] * SLOTS, [0] * SLOTS
    for ld in loads:
        s = min(range(SLOTS), key=lambda i: (-1,) if owner[i] is None else owner[i]["key"])
        ld["slot"], ld["before"] = s, owner[s]
        owner[s] = ld
        count[s] += 1
        ld["landed"] = 16 * count[s]
    return loads


def adds(n):
    R, J = divmod(n, NC)
    return (NC - 1) * R + (J if J == 1 else max(J - 1, 0))


LOADS = plan_phase_a()
SUMMED = [ld for ld in LOADS if ld["reduced"]]
ROWBLK = {(ld["r"], ld["J"]): ld for ld in LOADS if ld["row"]}
COLBLK = {(ld["r"], ld["J"]): ld for ld in LOADS if ld["col"]}
N_ROW, N_COL = len(ROWBLK), len(COLBLK)
A_HALVES = 2 * N_COL
C_CHUNKS = NC - SCH
C_HALVES = 2 * NC * C_CHUNKS
TURNS = [("C", c, J) for c in range(SCH, NC) for J in range(NC)]
TURNS += [("D", 0, J) for J in range(NC - 1)] + [("D", 1, J) for J in range(3)] + [("D", 0, NC - 1)]
TURNS += [("D", 1, J) for J in range(3, NC)]
D_START = TURNS.index(("D", 0, 0))
HOLD = TURNS.index(("D", 0, NC - 1))
FIRST_HI = 3
STAGE = {0: dict(add=13, v=15, w2=15, x1=17, x3=21, lo=22)}
STAGE.update({c: dict(add=8 * c + 12, v=8 * c + 14, w2=8 * c + 14, x1=8 * c + 16, x3=8 * c + 20, lo=8 * c + 21)
              for c in range(1, 4)})
STAGE[4] = dict(add=40, v=42, w2=42, x1=44, x3=47, lo=48)
STAGE[5] = dict(add=44, v=46, w2=46, x1=48, x3=50, lo=51)
STAGE[6] = dict(add=48, v=50, w2=50, x1=52, x3=54, lo=54)
STAGE[7] = dict(add=53, v=55, w2=55, x1=56, x3=58, lo=58)
LN_BEFORE = [(3, 0), (4, 1), (5, 2), (7, 0), (7, 2)] + [None] * 3
WEIGH = {(0, q): 12 + 3 * q for q in range(SUB)}
WEIGH.update({(c, q): 16 * c + 8 + 4 * q for c in range(1, 4) for q in range(SUB)})
WEIGH.update({(4 + i // SUB, i % SUB): 2 * g for i, g in enumerate(
    (36, 37, 38, 39, 40, 41, 42, 43, 44, 45, 46, 47, 49, 50, 51, 52))})
XB_BEFORE = {NC - 2: (2, 0), NC - 1: (1, 4)}


def due(stage, g):
    return [c for c in range(NC) if STAGE[c][stage] == g]


def weighs(g, hf):
    ops = []
    for (c, q), start in WEIGH.items():
        steps = ((1,), (2,), (3,)) if c < 4 else ((1,), (2, 3))
        if 0 <= 2 * g + hf - start < len(steps):
            ops += [(c, q, k) for k in steps[2 * g + hf - start]]
    return ops


def build(nc, x, at, w1, b1, w2, b2, w3, out):
    with ExitStack() as ctx:
        def sb(name, shape, dt=F32, stack=ctx):
            return stack.enter_context(nc.sbuf_tensor(name, shape, dt))

        def sem(name):
            return ctx.enter_context(nc.semaphore(name))

        h = sb("h", [P, NR, D])
        ut = sb("ut", [P, 2, CH])
        zt = sb("zt", [P, 2, SUB, D])
        negsq = sb("negsq", [P, N], BF16)
        x2s = sb("x2s", [P, GRP, D])
        with ExitStack() as over_z:
            near_odd = sb("near_odd", [P, SUB, D], F32, over_z)
        zslot = sb("zslot", [P, 2, 2, P], F32R)
        w1s, w2s, w3s = (sb(n, [D, D]) for n in ("w1s", "w2s", "w3s"))
        b1s, b2s = sb("b1s", [P, D]), sb("b2s", [P, D])
        ident = sb("ident", [P, P])
        ident16 = sb("ident16", [P, P], BF16)
        ones16 = sb("ones16", [P, P], BF16)
        ones = sb("ones", [P, 1])
        neghalf = sb("neghalf", [P, NR])
        poshalf = sb("poshalf", [P, K])
        stats = sb("stats", [P, NR, 6])
        meanvar = sb("meanvar", [P, NR, 2])
        vareps = sb("vareps", [P, NR])
        rstd = sb("rstd", [P, NR])
        negmean = sb("negmean", [P, NR])
        shift = sb("shift", [P, NR])
        deg = sb("deg", [P, NR])
        dis = sb("dis", [P, NR])
        sq = sb("sq", [P, NR])
        sqv = sb("sqv", [P, 3, NR])
        sqp = sb("sqp", [P, 3, NR], BF16)
        dis2 = sb("dis2", [P, NR])
        putby = sb("putby", [P, SUB])
        s4 = sb("s4", [P, NR, K])
        idx = sb("idx", [P, NR, K], U32)
        top = sb("top", [P, GRP, 8])
        topi = sb("topi", [P, GRP, 8], U32)
        dist = sb("dist", [P, GRP, 4, K])
        ssum = sb("ssum", [P, GRP])
        deg2 = sb("deg2", [P, GRP])
        idxs = sb("idxs", [P, 2 * SUB, K], U32)
        lnstat = sb("lnstat", [P, SUB, 6])
        lnmv = sb("lnmv", [P, SUB, 2])
        lnsc = sb("lnsc", [P, 5, SUB])

        with ExitStack() as a:
            xp = sb("xp", [P, NR, D], F32, a)
            part = sb("part", [P, PARTS, CH], F32, a)
            xst = sb("xst", [P, 2, 2, CH], F32R, a)
            split_a = sb("split_a", [P, DEPTH_A, 2, HALF], F32R, a)
            blk = sb("blk", [P, SLOTS, SUB, CH], F32, a)
        with ExitStack() as over_pan:
            even = []
            for i in range(2):
                sb(f"pan_head{i}", [P, (NC - 2) * CH], F32, over_pan)
                even.append(sb(f"xg_even{i}", [P, 2, K, D], F32, over_pan))
        pan = [sb("pan_hi", [P, N], F32R), sb("pan_lo", [P, N], F32R)]
        with ExitStack() as over_x2:
            spare = [sb(f"spare{i}", [P, SPARE, SUB // 2, CH], F32, over_x2) for i in range(2)]
        x2p = [sb("x2_hi", [P, N], F32R), sb("x2_lo", [P, N], F32R)]
        ring = sb("ring", [P, RING, SUB, CH])
        with ExitStack() as s:
            score = sb("score", [P, 2, N], F32, s)
        split_d = sb("split_d", [P, DEPTH_D, 2, HALF], F32R)
        odd = negsq[:, :].bitcast(F32).rearrange("p (q k f) -> p q k f", q=SUB, k=K)
        near = [[x2s[:, SUB + q, :] for q in range(SUB)],
                [near_odd[:, q, :] for q in range(SUB)]]

        def xg(c, q, k):
            return odd[:, q, k, :] if c % 2 else even[q % 2][:, q // 2, k, :]

        ps = ctx.enter_context(nc.psum_tensor("ps", [P, NC, CH], F32))
        x2d = nc.dram_tensor("x2_rows", (N, D), F32, kind="Internal").ap()

        x_in, w_in, b_in, xb_in = (sem(n) for n in ("x_in", "w_in", "b_in", "xb_in"))
        blk_in = [sem(f"blk_in{i}") for i in range(SLOTS)]
        spare_in = [sem(f"spare_in{i}") for i in range(SPARE)]
        ring_in = [sem(f"ring_in{i}") for i in range(RING)]
        consts, ident_z, ident_ok = sem("consts"), sem("ident_z"), sem("ident_ok")
        stats_ok, mv_ok, ln_step, ln_ok, h_ok = (sem(n) for n in ("stats_ok", "mv_ok", "ln_step", "ln_ok", "h_ok"))
        summed, added, deg_mm, deg_ok, dis_ok = (sem(n) for n in ("summed", "added", "deg_mm", "deg_ok", "dis_ok"))
        xp_ok, xhi_ok, xlo_ok = (sem(n) for n in ("xp_ok", "xhi_ok", "xlo_ok"))
        hi_made, lo_made, split_used = (sem(n) for n in ("hi_made", "lo_made", "split_used"))
        row_done, room_made, restored = sem("row_done"), sem("room_made"), sem("restored")
        u_ok, zw_mm, zt_part, z_ok, sq_ok = (sem(n) for n in ("u_ok", "zw_mm", "zt_part", "z_ok", "sq_ok"))
        zt_mm, zhi_ok, zlo_ok, sqv_ok, sqp_mm, negsq_ok = (
            sem(n) for n in ("zt_mm", "zhi_ok", "zlo_ok", "sqv_ok", "sqp_mm", "negsq_ok"))
        zslot_ok, zz_mm, score_ok, top_ok, topi_ok = (
            sem(n) for n in ("zslot_ok", "zz_mm", "score_ok", "top_ok", "topi_ok"))
        dist_ok, s4_ok, deg2_ok, dis2_ok, x2_ok, x2hi_ok, x2lo_ok, x2_used, idx_ok = (
            sem(n) for n in ("dist_ok", "s4_ok", "deg2_ok", "dis2_ok", "x2_ok", "x2hi_ok", "x2lo_ok",
                             "x2_used", "idx_ok"))
        x2_out = [sem("x2_out0"), sem("x2_out1")]
        idxs_ok, gathered, weigh0, weighed, g_mm = (
            sem("idxs_ok"), [sem(f"gathered{q}") for q in range(2 * SUB)], sem("weigh0"), sem("weighed"), sem("g_mm"))
        v_ok, w2_mm, x1_ok, lnst_ok, lnmv_ok, lnsc_ok, x3_ok, x3hi_ok, x3lo_ok, xb_ok = (
            sem(n) for n in ("v_ok", "w2_mm", "x1_ok", "lnst_ok", "lnmv_ok", "lnsc_ok",
                             "x3_ok", "x3hi_ok", "x3lo_ok", "xb_ok"))
        t_ok, w3_mm, y_ok = (sem(n) for n in ("t_ok", "w3_mm", "y_ok"))
        waited = sem("waited")
        y_sent = [sem("y_sent0"), sem("y_sent1")]

        def static(v):
            return isinstance(v, int)

        def out_chunk(k):
            return NC - 1 if static(k) and k == 0 else k - 1

        def wait_apart(eng, signal, value):
            eng.wait_ge(signal, value)
            eng.sem_inc(waited)

        block = ctx.enter_context(nc.Block())

        @block.sync
        def _(sp):
            sp.dma_start(xp[:, :, :], x[:, :, :]).then_inc(x_in, 16)

            for n, ld in enumerate(LOADS):
                old = ld["before"]
                if n == 2:
                    for dst, src in ((w1s, w1), (w2s, w2), (w3s, w3)):
                        sp.dma_start(dst[:, :], src[:, :]).then_inc(w_in, 16)
                    for dst, src in ((b1s, b1), (b2s, b2)):
                        row = src.rearrange("(a f) -> a f", a=1)
                        sp.dma_start(dst[:, :], row.broadcast_to([P, D])).then_inc(b_in, 16)
                if old is not None:
                    if old["reduced"]:
                        sp.wait_ge(summed, old["reduced"])
                    if old["row"]:
                        sp.wait_ge(row_done, old["row"])
                    if old["col"]:
                        sp.wait_ge(lo_made, 2 * old["col"])
                sp.dma_start(blk[:, ld["slot"], :, :], at[ld["r"], ld["J"]]).then_inc(blk_in[ld["slot"]], 16)

            sp.wait_ge(lo_made, A_HALVES)
            sp.wait_ge(split_used, A_HALVES)

            def load_s(J, half):
                for c in range(SCH):
                    slot = SUB + 2 * half + c
                    sp.dma_start(ring[:, slot, :, :], at[c, J]).then_inc(ring_in[slot], 16)

            load_s(0, 0)
            load_s(1, 1)
            for J in range(SUB):
                sp.dma_start(ring[:, J, :, :], at[SCH, J]).then_inc(ring_in[J], 16)
            with sp.Fori(0, NC // 2 - 1) as it:
                for half in range(2):
                    sp.wait_ge(x2_used, it * GRP + SUB * (half + 1))
                    for c in range(SCH):
                        slot = SUB + 2 * half + c
                        sp.dma_start(ring[:, slot, :, :], at[c, ds(it * 2 + (2 + half), 1)].rearrange(
                            "a p s c -> (a p) s c")).then_inc(ring_in[slot], 16)
            for half in range(2):
                sp.wait_ge(x2_used, NR - SUB * (2 - half) + SUB)
                for c in range(SCH):
                    slot = SUB + 2 * half + c
                    sp.dma_start(ring[:, slot, :, :], at[SCH, slot]).then_inc(ring_in[slot], 16)
            sp.dma_start(zt[:, 0, :, :], x[:, 0:SUB, :]).then_inc(xb_in, 16)
            for g in range(NC, D_START):
                for c in due("x1", g + 4):
                    if c:
                        sp.wait_ge(xb_ok, c)
                        sp.dma_start(zt[:, 0, :, :], x[:, c * SUB:(c + 1) * SUB, :]).then_inc(xb_in, 16)
                _, c, J = TURNS[g]
                sp.wait_ge(lo_made, A_HALVES + 2 * (g - NC) + 2)
                sp.dma_start(ring[:, J, :, :], at[c, J]).then_inc(ring_in[J], 16)

            def load_d(k, J):
                if k == 1 and J < SPARE:
                    sp.wait_ge(split_used, A_HALVES + 2 * TURNS.index(("C", NC - 1, 2 * J + 1)) + 2)
                    for i in range(2):
                        sp.dma_start(spare[i][:, J, :, :],
                                     at[0, J][:, i * (SUB // 2):(i + 1) * (SUB // 2), :]).then_inc(spare_in[J], 16)
                else:
                    last = ("D", 0 if k == 1 or J < SPARE else 1, J)
                    sp.wait_ge(lo_made, A_HALVES + 2 * TURNS.index(last) + 2)
                    sp.dma_start(ring[:, J, :, :], at[k - 1, J]).then_inc(ring_in[J], 16)

            for J in range(SPARE):
                load_d(1, J)
            for k, J in [(2, J) for J in range(SPARE)] + [(1, J) for J in range(SPARE, NC)] + [
                    (2, J) for J in range(SPARE, NC)]:
                for c in range(NC - 2, NC):
                    if XB_BEFORE[c] == (k, J):
                        sp.wait_ge(xb_ok, c)
                        sp.dma_start(zt[:, 0, :, :], x[:, c * SUB:(c + 1) * SUB, :]).then_inc(xb_in, 16)
                load_d(k, J)
            with sp.Fori(3, NC) as k:
                for J in range(NC):
                    sp.wait_ge(lo_made, k * (2 * NC) + (A_HALVES + C_HALVES - 2 * NC + 2 * J + 2))
                    sp.dma_start(ring[:, J, :, :], at[ds(k - 1, 1), J].rearrange(
                        "a p s c -> (a p) s c")).then_inc(ring_in[J], 16)
            sp.wait_ge(y_sent[0], 16 * NC // 2)
            sp.wait_ge(y_sent[1], 16 * NC // 2)

        def half_of(phase, c, J, hf):
            spared = (phase, c) == ("D", 1) and J < SPARE
            half = spare[hf][:, J, :, :] if spared else ring[:, J, 2 * hf:2 * hf + 2, :]
            return half.rearrange("p a c -> p (a c)")

        def ring_landed(eng, J, loads_before):
            base = NC // 2 if J >= SUB else 0
            eng.wait_ge(ring_in[J], loads_before * 16 + 16 * (base + 1))

        @block.tensor
        def _(pe):
            def split_half(bank, n, hf, w, wcol, first, last, slot=0):
                in_a = static(n) and n < A_HALVES
                part_of = split_a[:, n % DEPTH_A] if in_a else split_d[:, slot]
                for sub in range(SUB // 2):
                    c0 = wcol + (hf * (SUB // 2) + sub) * P
                    for g, (wi, ai) in enumerate(((0, 0), (1, 0), (0, 1))):
                        mm = pe.matmul(ps[:, bank, :] if static(bank) else
                                       ps[:, ds(bank, 1), :].rearrange("p a c -> p (a c)"),
                                       w[wi][:, c0:c0 + P],
                                       part_of[:, ai, sub * CH:(sub + 1) * CH],
                                       start=first and sub == 0 and g == 0,
                                       stop=last and sub == SUB // 2 - 1 and g == 2, skip_group_check=True)
                return mm

            def deg_sum(R):
                pe.wait_ge(added, adds(NC * (R + 1)))
                if R == 0:
                    pe.wait_ge(consts, 1)
                if R == NC - 1:
                    pe.wait_ge(room_made, 2)
                for q in range(SUB):
                    to = ps[:, 0, q:q + 1] if R == NC - 1 else ps[:, NC - 1, R * SUB + q:R * SUB + q + 1]
                    mm = pe.matmul(to, ut[:, R % 2, q * P:(q + 1) * P], ones[:, :], start=R < NC - 1,
                                   stop=R < NC - 1, skip_group_check=True)
                mm.then_inc(deg_mm, 1)

            def row_block(R, J):
                ld = ROWBLK[R, J]
                pe.wait_ge(blk_in[ld["slot"]], ld["landed"])
                pe.wait_ge(xp_ok, SUB * (J + 1))
                if (R, J) == (NC - 1, 0):
                    pe.wait_ge(deg_ok, NC - 1)
                for sub in range(SUB):
                    mm = pe.matmul(ps[:, R, :], xp[:, J * SUB + sub, :], blk[:, ld["slot"], sub, :],
                                   start=(J == 0 and sub == 0), stop=False, skip_group_check=True)
                mm.then_inc(row_done, 1)

            def col_block(r, J):
                ld = COLBLK[r, J]
                if r == 0:
                    pe.wait_ge(xlo_ok, J + 1)
                    if J == NC - 1:
                        pe.wait_ge(restored, 1)
                for hf in range(2):
                    n = 2 * (ld["col"] - 1) + hf
                    pe.wait_ge(lo_made, n + 1)
                    split_half(r, n, hf, [xst[:, J % 2, 0, :], xst[:, J % 2, 1, :]], 0,
                               J == 0 and hf == 0, J == NC - 1 and hf == 1).then_inc(split_used, 1)

            def z_rows(c):
                pe.wait_ge(u_ok, c + 1)
                pe.wait_ge(w_in, 48)
                for q in range(SUB):
                    mm = pe.matmul(ps[:, c, q * D:(q + 1) * D], ut[:, c % 2, q * P:(q + 1) * P], w1s[:, :],
                                   start=True, stop=True, skip_group_check=True)
                mm.then_inc(zw_mm, 1)

            def z_turn(c):
                pe.wait_ge(z_ok, c + 1)
                for q in range(SUB):
                    mm = pe.transpose(ps[:, c, q * P:(q + 1) * P], zt[:, c % 2, q, :], ident[:, :])
                mm.then_inc(zt_mm, 1)

            for R in range(NC):
                for J, rs in stage(R):
                    if J is None:
                        deg_sum(R)
                    elif J < R:
                        row_block(R, J)
                    for r in rs:
                        col_block(r, R - 1)
                if R == 0:
                    deg_sum(0)

            def spread_negsq(g):
                pe.wait_ge(sqv_ok, 6 * (g + 1))
                pe.wait_ge(ident_ok, 2)
                pe.wait_ge(zlo_ok, 2 * g + 2)
                for r in range(2 * SUB * g, 2 * SUB * (g + 1)):
                    mm = pe.matmul(ps[0:3, r // SUB, (r % SUB) * P:(r % SUB + 1) * P], sqp[:, :, r], ident16[:, :],
                                   start=True, stop=True, skip_group_check=True)
                mm.then_inc(sqp_mm, 1)

            def zz_unit(r, u, q, bank0):
                for b in range(2):
                    cols = slice((2 * q + b) * CH, (2 * q + b + 1) * CH)
                    pe.matmul(ps[:, bank0 + b, :], ones16[:, :], negsq[:, cols], start=True, stop=False)
                    for g, (wi, mi) in enumerate(((0, 0), (1, 0), (0, 1))):
                        mm = pe.matmul(ps[:, bank0 + b, :], zslot[:, u % 2, wi, :], pan[mi][:, cols],
                                       start=False, stop=(g == 2))
                mm.then_inc(zz_mm, 1)

            pe.wait_ge(ident_ok, 1)
            for t in range(Z_TURNS):
                if t < NC:
                    col_block(t, NC - 1)
                if 0 <= t - Z["rows"] < NC:
                    z_rows(t - Z["rows"])
                if 0 <= t - Z["turn"] < NC:
                    z_turn(t - Z["turn"])
                if t - NEG["spread"] in range(1, NC, 2):
                    spread_negsq((t - NEG["spread"]) // 2)
                if t in FIRST_SCORES:
                    q = FIRST_SCORES.index(t)
                    if q == 0:
                        pe.wait_ge(consts, 1)
                        pe.wait_ge(zslot_ok, 2)
                    pe.wait_ge(negsq_ok, q + 1)
                    zz_unit(0, 0, q, 2 * q)
            def zz(r, u):
                pe.wait_ge(zslot_ok, 2 * r + 2)
                for q in range(4):
                    pe.wait_ge(score_ok, r * 4 + q - 1)
                    zz_unit(r, u, q, 4 + 2 * (q % 2))

            def product_s(r, u, it):
                if u % SUB == 0:
                    for c in range(SCH):
                        slot = SUB + 2 * (u // SUB) + c
                        pe.wait_ge(ring_in[slot], it * 16 + 16)
                pe.wait_ge(x2_ok, r + 1)
                for c in range(SCH):
                    mm = pe.matmul(ps[:, c, :], x2s[:, u, :], ring[:, SUB + 2 * (u // SUB) + c, u % SUB, :],
                                   start=static(r) and r == 0, stop=False, skip_group_check=True)
                mm.then_inc(x2_used, 1)

            zz(1, 1)
            for u in range(GRP):
                zz(u + 2, u)
                if u:
                    product_s(u - 1, u - 1, 0)
            with pe.Fori(1, NR // GRP - 1) as it:
                for u in range(GRP):
                    zz(it * GRP + (u + 2), u)
                    product_s(it * GRP + (u - 1), (u - 1) % GRP, it)
            for u in range(GRP):
                r = NR - GRP + u
                if r + 2 < NR:
                    zz(r + 2, u)
                product_s(r - 1, (u - 1) % GRP, NR // GRP - 1)

            def product(bank, n0, panels, J):
                for hf in range(2):
                    pe.wait_ge(lo_made, n0 + (2 * J + hf + 1))
                    mm = split_half(bank, n0, hf, panels, J * CH, J == 0 and hf == 0, False, (2 * J + hf) % DEPTH_D)
                    mm.then_inc(split_used, 1)
                return mm

            def bank_of(c):
                return ps[:, c, :] if static(c) else ps[:, ds(c, 1), :].rearrange("p a c -> p (a c)")

            def add_neighbours(c):
                for q in range(SUB):
                    pe.wait_ge(weighed, (K - 1) * (c * SUB + q + 1))
                    mm = pe.matmul(bank_of(c)[:, q * P:(q + 1) * P], near[c % 2][q], ident[:, :],
                                   start=False, stop=(q == SUB - 1), skip_group_check=True)
                    mm.then_inc(g_mm, 1)

            def rows_w(c, w, ready, parity_col, done):
                pe.wait_ge(ready, c + 1)
                for q in range(SUB):
                    mm = pe.matmul(bank_of(c)[:, q * D:(q + 1) * D], ut[:, parity_col, q * P:(q + 1) * P], w[:, :],
                                   start=True, stop=True, skip_group_check=True)
                mm.then_inc(done, 1)

            x2w = [x2p[0][:, :], x2p[1][:, :]]
            panw = [pan[0][:, :], pan[1][:, :]]
            for g, (phase, c, J) in enumerate(TURNS):
                if phase == "D":
                    pe.wait_ge(x3lo_ok, J + 1)
                if g < NC:
                    pe.wait_ge(x2lo_ok, SUB * (J + 1))
                for hf in range(2):
                    n = 2 * g + hf
                    pe.wait_ge(lo_made, A_HALVES + n + 1)
                    split_half(c, A_HALVES + n, hf, x2w if phase == "C" else panw, J * CH, J == 0 and hf == 0, False,
                               n % DEPTH_D).then_inc(split_used, 1)
                if g == 0:
                    product_s(NR - 1, GRP - 1, NR // GRP - 1)
                for ch in due("add", g):
                    add_neighbours(ch)
                for ch in due("w2", g):
                    rows_w(ch, w2s, v_ok, 0, w2_mm)
                if g == HOLD + 2:
                    rows_w(0, w3s, t_ok, 1, w3_mm)
            with pe.Fori(2, NC) as k:
                n0 = k * (2 * NC) + (A_HALVES + C_HALVES)
                for J in range(NC):
                    product(k, n0, panw, J)
                    if J == 1:
                        rows_w(k - 1, w3s, t_ok, 1, w3_mm)
            rows_w(NC - 1, w3s, t_ok, 1, w3_mm)

        @block.scalar
        def _(act):
            def hi_half(src, buf, slot):
                nc.scalar.activation(buf[:, slot, 0, :], src, ACT.Copy).then_inc(hi_made, 1)

            act.wait_ge(ln_ok, 1)
            for r in range(NR):
                nc.scalar.activation(h[:, r, :], xp[:, r, :], ACT.Relu, bias=shift[:, r:r + 1],
                                     scale=rstd[:, r:r + 1]).then_inc(h_ok, 1)

            def u_copy(c):
                act.wait_ge(split_used, 2 * COLBLK[c, NC - 1]["col"])
                if c >= 2:
                    act.wait_ge(zw_mm, c - 1)
                nc.scalar.copy(ut[:, c % 2, :], ps[:, c, :]).then_inc(u_ok, 1)

            def z_squares(c):
                act.wait_ge(z_ok, c + 1)
                if c:
                    act.wait_ge(sq_ok, SUB * c)
                for q in range(SUB):
                    nc.scalar.activation(x2s[:, q, :], zt[:, c % 2, q, :], ACT.Square,
                                         accum_out=sq[:, c * SUB + q:c * SUB + q + 1]).then_inc(sq_ok, 1)

            def z_hi(c):
                act.wait_ge(zt_mm, c + 1)
                act.wait_ge(row_done, N_ROW)
                nc.scalar.activation(pan[0][:, c * CH:(c + 1) * CH], ps[:, c, :], ACT.Copy).then_inc(zhi_ok, 1)

            def hi_col(r, J, hf):
                ld = COLBLK[r, J]
                n = 2 * (ld["col"] - 1) + hf
                act.wait_ge(blk_in[ld["slot"]], ld["landed"])
                if n >= DEPTH_A:
                    act.wait_ge(split_used, n - DEPTH_A + 1)
                hi_half(blk[:, ld["slot"], 2 * hf:2 * hf + 2, :].rearrange("p a c -> p (a c)"), split_a, n % DEPTH_A)

            for R in range(NC):
                for r in [r for _, rs in stage(R) for r in rs]:
                    hi_col(r, R - 1, 0)
                    hi_col(r, R - 1, 1)
                act.wait_ge(xp_ok, SUB * (R + 1))
                if R >= 2:
                    act.wait_ge(split_used, 2 * COLBLK[R - 2, R - 2]["col"])
                nc.scalar.activation(xst[:, R % 2, 0, :], xp[:, R * SUB:(R + 1) * SUB, :].rearrange("p a f -> p (a f)"),
                                     ACT.Copy).then_inc(xhi_ok, 1)
            def copy_unit(r, u, q, bank0):
                act.wait_ge(zz_mm, r * 4 + (q + 1))
                nc.scalar.copy(score[:, u % 2, 2 * q * CH:(2 * q + 2) * CH],
                               ps[:, bank0:bank0 + 2, :].rearrange("p a c -> p (a c)")).then_inc(score_ok, 1)

            for t in range(Z_TURNS):
                if t < NC:
                    hi_col(t, NC - 1, 0)
                if 0 <= t - Z["u"] < NC:
                    u_copy(t - Z["u"])
                if 0 <= t - Z["squares"] < NC:
                    z_squares(t - Z["squares"])
                if t < NC:
                    hi_col(t, NC - 1, 1)
                if 0 <= t - Z["hi"] < NC:
                    z_hi(t - Z["hi"])
                if t - NEG["copy"] in range(1, NC, 2):
                    g = (t - NEG["copy"]) // 2
                    act.wait_ge(ident_ok, 3)
                    act.wait_ge(sqp_mm, g + 1)
                    nc.scalar.copy(negsq[0:3, 2 * g * CH:(2 * g + 2) * CH],
                                   ps[0:3, 2 * g:2 * g + 2, :].rearrange("p a c -> p (a c)")).then_inc(negsq_ok, 1)
                if t in FIRST_COPIES:
                    if t == FIRST_COPIES[0]:
                        act.wait_ge(lo_made, A_HALVES)
                    copy_unit(0, 0, FIRST_COPIES.index(t), 2 * FIRST_COPIES.index(t))

            def copy_scores(r, u):
                if not (static(r) and r < 2):
                    act.wait_ge(topi_ok, r - 1)
                for q in range(4):
                    copy_unit(r, u, q, 4 + 2 * (q % 2))

            def row(t, r):
                return t[:, r, :] if static(r) else t[:, ds(r, 1), :].rearrange("p a f -> p (a f)")

            def col(t, r):
                return t[:, r:r + 1] if static(r) else t[:, ds(r, 1)]

            def panel(t, r):
                return t[:, r * P:(r + 1) * P] if static(r) else t[:, ds(r * P, P)]

            def neighbours(r, u):
                act.wait_ge(dist_ok, 4 * r + 4)
                nc.scalar.activation(row(s4, r), dist[:, u, 3, :], ACT.Exp, scale=-0.5,
                                     accum_out=ssum[:, u:u + 1]).then_inc(s4_ok, 1)
                act.wait_ge(dis2_ok, r + 1)
                nc.scalar.activation(x2s[:, u, :], row(h, r), ACT.Copy, scale=col(dis2, r)).then_inc(x2_ok, 1)
                nc.scalar.activation(panel(x2p[0], r), row(h, r), ACT.Copy, scale=col(dis2, r)).then_inc(x2hi_ok, 1)
                act.wait_ge(x2_ok, r + 1)
                act.dma_start(x2d[r * P:(r + 1) * P, :] if static(r) else x2d[ds(r * P, P), :],
                              x2s[:, u, :]).then_inc(x2_out[u // SUB], 16)

            act.wait_ge(sq_ok, NR)

            def turn_s(it):
                for u in range(GRP):
                    r = it * GRP + u
                    if not (static(it) and r + 1 == NR):
                        copy_scores(r + 1, u + 1)
                    if u % SUB == 1 and not (static(it) and it == 0):
                        act.wait_ge(x2_out[u // SUB], it * (16 * SUB))
                    if not (static(it) and r == 0):
                        neighbours(r - 1, (u - 1) % GRP)

            turn_s(0)
            with act.Fori(1, NR // GRP - 1) as it:
                turn_s(it)
            turn_s(NR // GRP - 1)

            def hi_block(n0, J, loads_before):
                ring_landed(act, J, loads_before)
                for hf in range(2):
                    act.wait_ge(split_used, n0 + (2 * J + hf - DEPTH_D + 1))
                    hi_half(ring[:, J, 2 * hf:2 * hf + 2, :].rearrange("p a c -> p (a c)"), split_d,
                            (2 * J + hf) % DEPTH_D)

            def bank_of(c):
                return ps[:, c, :] if static(c) else ps[:, ds(c, 1), :].rearrange("p a c -> p (a c)")

            def v_copy(c):
                act.wait_ge(g_mm, c * SUB + SUB)
                if not (static(c) and c == 0):
                    act.wait_ge(w2_mm, c)
                nc.scalar.copy(ut[:, 0, :], bank_of(c)).then_inc(v_ok, 1)

            def x3(c):
                act.wait_ge(lnsc_ok, c * 5 + 5)
                if not (static(c) and c == 0):
                    act.wait_ge(x3lo_ok, c)
                for q in range(SUB):
                    nc.scalar.activation(x2s[:, q, :], row(h, c * SUB + q), ACT.Relu, bias=lnsc[:, 4, q:q + 1],
                                         scale=lnsc[:, 2, q:q + 1]).then_inc(x3_ok, 1)
                act.wait_ge(x3_ok, c * SUB + SUB)
                nc.scalar.activation(pan[0][:, c * CH:(c + 1) * CH] if static(c) else pan[0][:, ds(c * CH, CH)],
                                     x2s[:, 0:SUB, :].rearrange("p a f -> p (a f)"), ACT.Copy).then_inc(x3hi_ok, 1)

            def t_copy(c):
                act.wait_ge(split_used, A_HALVES + 2 * HOLD + 2 if static(c) and c == 0 else
                            c * (2 * NC) + (A_HALVES + C_HALVES + 2 * NC))
                if not (static(c) and c == 0):
                    act.wait_ge(w3_mm, c)
                nc.scalar.copy(ut[:, 1, :], bank_of(c)).then_inc(t_ok, 1)

            act.wait_ge(topi_ok, NR - 1)
            def weigh_first(c, q):
                r = c * SUB + q
                if c >= 2:
                    act.wait_ge(g_mm, r - 2 * SUB + 1)
                act.wait_ge(gathered[r % (2 * SUB)], 16 * K * (c // 2 + 1))
                nc.scalar.activation(near[c % 2][q], xg(c, q, 0), ACT.Copy, scale=s4[:, r, 0:1]).then_inc(weigh0, 1)

            for g, (phase, c, J) in enumerate(TURNS):
                if (phase, c) == ("D", 1) and J < SPARE:
                    act.wait_ge(spare_in[J], 32)
                else:
                    ring_landed(act, J, c - SCH if phase == "C" else C_CHUNKS - 1 + c)
                for hf in range(2):
                    n = 2 * g + hf
                    if n == DEPTH_D // 2:
                        act.wait_ge(topi_ok, NR)
                    if n == FIRST_HI:
                        neighbours(NR - 1, GRP - 1)
                    act.wait_ge(split_used, A_HALVES + n - DEPTH_D + 1)
                    hi_half(half_of(phase, c, J, hf), split_d, n % DEPTH_D)
                for (ch, q), start in WEIGH.items():
                    if start // 2 == g + 1:
                        weigh_first(ch, q)
                for ch in due("v", g):
                    v_copy(ch)
                for ch in due("x3", g):
                    x3(ch)
                if g == HOLD + 2:
                    t_copy(0)

            with act.Fori(2, NC) as k:
                n0 = k * (2 * NC) + (A_HALVES + C_HALVES)
                for J in range(NC):
                    hi_block(n0, J, k + (C_CHUNKS - 2 if J < SPARE else C_CHUNKS - 1))
                    if J == 0:
                        t_copy(k - 1)
            t_copy(NC - 1)

        @block.vector
        def _(dve):
            def lo_half(src, buf, slot):
                nc.vector.tensor_tensor(buf[:, slot, 1, :], src, buf[:, slot, 0, :].bitcast(F32),
                                        ALU.subtract).then_inc(lo_made, 1)

            dve.wait_ge(x_in, 16)
            for r in range(NR):
                nc.vector.bn_stats(stats[:, r, :], xp[:, r, :]).then_inc(stats_ok, 1)
            dve.wait_ge(stats_ok, NR)
            for r in range(NR):
                nc.vector.bn_aggr(meanvar[:, r, :], stats[:, r, :]).then_inc(mv_ok, 1)

            def z_make(c):
                dve.wait_ge(zw_mm, c + 1)
                dve.wait_ge(b_in, 32)
                if c >= 2:
                    dve.wait_ge(zt_mm, c - 1)
                    dve.wait_ge(sq_ok, SUB * (c - 1))
                for q in range(SUB):
                    r = c * SUB + q
                    nc.vector.scalar_tensor_tensor(zt[:, c % 2, q, :], ps[:, c, q * D:(q + 1) * D], dis[:, r:r + 1],
                                                   b1s[:, :], ALU.mult, ALU.add).then_inc(zt_part, 1)
                dve.wait_ge(zt_part, SUB * (c + 1))
                zz = zt[:, c % 2, :, :].rearrange("p q f -> p (q f)")
                nc.vector.scalar_tensor_tensor(zz, zz, SLOPE, zz, ALU.mult, ALU.max).then_inc(z_ok, 1)

            def z_lo(c):
                dve.wait_ge(zhi_ok, c + 1)
                nc.vector.tensor_tensor(pan[1][:, c * CH:(c + 1) * CH], ps[:, c, :],
                                        pan[0][:, c * CH:(c + 1) * CH].bitcast(F32), ALU.subtract).then_inc(zlo_ok, 1)

            def degree_sum(n):
                ld = SUMMED[n]
                dve.wait_ge(blk_in[ld["slot"]], ld["landed"])
                if n >= PARTS:
                    dve.wait_ge(added, adds(n - PARTS + 1))
                nc.vector.tensor_reduce(part[:, n % PARTS, :], blk[:, ld["slot"], :, :].rearrange("p s c -> p c s"),
                                        AX_X, ALU.add).then_inc(summed, 1)

            bank0 = ps[:, 0, 0:SUB]
            def lo_col(r, J):
                ld = COLBLK[r, J]
                for hf in range(2):
                    n = 2 * (ld["col"] - 1) + hf
                    dve.wait_ge(hi_made, n + 1)
                    lo_half(blk[:, ld["slot"], 2 * hf:2 * hf + 2, :].rearrange("p a c -> p (a c)"), split_a,
                            n % DEPTH_A)

            for R in range(NC):
                for i, (J, rs) in enumerate(stage(R)):
                    if J is not None:
                        degree_sum(NC * R + i)
                    if (R, i) == (NC - 1, NC - 1):
                        dve.wait_ge(split_used, 2 * COLBLK[0, NC - 2]["col"])
                        nc.vector.tensor_copy(putby[:, :], bank0).then_inc(room_made, 1)
                        dve.wait_ge(room_made, 1)
                        nc.vector.memset(bank0, 0.0).then_inc(room_made, 1)
                    for r in rs:
                        lo_col(r, R - 1)
                dve.wait_ge(deg_mm, R + 1)
                nc.vector.tensor_copy(deg[:, R * SUB:(R + 1) * SUB], bank0 if R == NC - 1 else
                                      ps[:, NC - 1, R * SUB:(R + 1) * SUB]).then_inc(deg_ok, 1)
                if R == NC - 1:
                    dve.wait_ge(deg_ok, NC)
                    nc.vector.tensor_copy(bank0, putby[:, :]).then_inc(restored, 1)
                dve.wait_ge(dis_ok, R + 1)
                if R == 0:
                    dve.wait_ge(h_ok, NR)
                for q in range(SUB):
                    r = R * SUB + q
                    nc.vector.tensor_scalar(xp[:, r, :], h[:, r, :], dis[:, r:r + 1], None, ALU.mult).then_inc(xp_ok, 1)
                dve.wait_ge(xhi_ok, R + 1)
                nc.vector.tensor_tensor(xst[:, R % 2, 1, :], xp[:, R * SUB:(R + 1) * SUB, :].rearrange("p a f -> p (a f)"),
                                        xst[:, R % 2, 0, :].bitcast(F32), ALU.subtract).then_inc(xlo_ok, 1)
            def negsq_parts(g):
                c = slice(2 * SUB * g, 2 * SUB * (g + 1))
                dve.wait_ge(sq_ok, 2 * SUB * (g + 1))
                nc.vector.tensor_scalar(sqv[:, 0, c], sq[:, c], -0.5, None, ALU.mult).then_inc(sqv_ok, 1)
                dve.wait_ge(sqv_ok, 6 * g + 1)
                for i in range(3):
                    nc.vector.tensor_copy(sqp[:, i, c], sqv[:, i, c]).then_inc(sqv_ok, 1)
                    dve.wait_ge(sqv_ok, 6 * g + 2 * i + 2)
                    if i < 2:
                        nc.vector.tensor_tensor(sqv[:, i + 1, c], sqv[:, i, c], sqp[:, i, c],
                                                ALU.subtract).then_inc(sqv_ok, 1)
                        dve.wait_ge(sqv_ok, 6 * g + 2 * i + 3)

            for t in range(Z_TURNS):
                if t < NC:
                    lo_col(t, NC - 1)
                if 0 <= t - Z["make"] < NC:
                    z_make(t - Z["make"])
                if 0 <= t - Z["lo"] < NC:
                    z_lo(t - Z["lo"])
                if t - NEG["parts"] in range(1, NC, 2):
                    negsq_parts((t - NEG["parts"]) // 2)

            with dve.Fori(0, NR // GRP) as it:
                for u in range(GRP):
                    r = it * GRP + u
                    wait_apart(dve, score_ok, r * 4 + 4)
                    nc.vector.max(top[:, u, :], score[:, u % 2, :]).then_inc(top_ok, 1)
                    wait_apart(dve, top_ok, r + 1)
                    nc.vector.max_index(topi[:, u, :], top[:, u, :], score[:, u % 2, :]).then_inc(topi_ok, 1)

            def lo_block(n0, J):
                for hf in range(2):
                    dve.wait_ge(hi_made, n0 + (2 * J + hf + 1))
                    lo_half(ring[:, J, 2 * hf:2 * hf + 2, :].rearrange("p a c -> p (a c)"), split_d,
                            (2 * J + hf) % DEPTH_D)

            def weigh(c, q, k):
                r = c * SUB + q
                if k == 1:
                    dve.wait_ge(weigh0, r + 1)
                else:
                    dve.wait_ge(weighed, r * (K - 1) + k - 1)
                acc = near[c % 2][q]
                nc.vector.scalar_tensor_tensor(acc, xg(c, q, k), s4[:, r, k:k + 1], acc,
                                               ALU.mult, ALU.add).then_inc(weighed, 1)

            def row(t, r):
                return t[:, r, :] if static(r) else t[:, ds(r, 1), :].rearrange("p a f -> p (a f)")

            def col(t, r):
                return t[:, r:r + 1] if static(r) else t[:, ds(r, 1)]

            def bank_of(c):
                return ps[:, c, :] if static(c) else ps[:, ds(c, 1), :].rearrange("p a c -> p (a c)")

            def x1_rows(c):
                dve.wait_ge(w2_mm, c + 1)
                dve.wait_ge(xb_ok, c + 1)
                for q in range(SUB):
                    r = c * SUB + q
                    nc.vector.scalar_tensor_tensor(h[:, r, :], ps[:, c, q * D:(q + 1) * D], dis2[:, r:r + 1],
                                                   zt[:, 1, q, :], ALU.mult, ALU.add).then_inc(x1_ok, 1)
                for q in range(SUB):
                    dve.wait_ge(x1_ok, c * SUB + q + 1)
                    nc.vector.bn_stats(lnstat[:, q, :], h[:, c * SUB + q, :]).then_inc(lnst_ok, 1)
                for q in range(SUB):
                    dve.wait_ge(lnst_ok, c * SUB + q + 1)
                    nc.vector.bn_aggr(lnmv[:, q, :], lnstat[:, q, :]).then_inc(lnmv_ok, 1)
                dve.wait_ge(lnmv_ok, c * SUB + SUB)
                if c:
                    dve.wait_ge(x3_ok, c * SUB)
                nc.vector.tensor_scalar(lnsc[:, 0, :], lnmv[:, :, 1], EPS, None, ALU.add).then_inc(lnsc_ok, 1)
                nc.vector.tensor_scalar(lnsc[:, 3, :], lnmv[:, :, 0], -1.0, None, ALU.mult).then_inc(lnsc_ok, 1)

            def x3_lo(c):
                dve.wait_ge(x3hi_ok, c + 1)
                hi = pan[0][:, c * CH:(c + 1) * CH] if static(c) else pan[0][:, ds(c * CH, CH)]
                lo = pan[1][:, c * CH:(c + 1) * CH] if static(c) else pan[1][:, ds(c * CH, CH)]
                nc.vector.tensor_tensor(lo, x2s[:, 0:SUB, :].rearrange("p a f -> p (a f)"), hi.bitcast(F32),
                                        ALU.subtract).then_inc(x3lo_ok, 1)

            def y_rows(k):
                dve.wait_ge(w3_mm, k + 1)
                for q in range(SUB):
                    r = out_chunk(k) * SUB + q
                    nc.vector.scalar_tensor_tensor(row(h, r), bank_of(k)[:, q * D:(q + 1) * D], col(dis, r),
                                                   row(h, r), ALU.mult, ALU.add).then_inc(y_ok, 1)

            dve.wait_ge(split_used, A_HALVES)
            for g, (phase, c, J) in enumerate(TURNS):
                for hf in range(2):
                    n = 2 * g + hf
                    dve.wait_ge(hi_made, A_HALVES + n + 1)
                    lo_half(half_of(phase, c, J, hf), split_d, n % DEPTH_D)
                    for op in weighs(g, hf):
                        weigh(*op)
                for ch in due("x1", g):
                    x1_rows(ch)
                for ch in due("lo", g):
                    x3_lo(ch)
                if g == HOLD + 3:
                    y_rows(0)
            with dve.Fori(2, NC) as k:
                n0 = k * (2 * NC) + (A_HALVES + C_HALVES)
                for J in range(NC):
                    lo_block(n0, J)
                    if J == 2:
                        y_rows(k - 1)
            y_rows(NC - 1)

        @block.gpsimd
        def _(pool):
            nc.gpsimd.memset(ones[:, :], 1.0)
            nc.gpsimd.memset(ones16[:, :], 1.0)
            nc.gpsimd.memset(neghalf[:, :], -0.5)
            nc.gpsimd.memset(poshalf[:, :], 0.5).then_inc(consts, 1)
            nc.gpsimd.memset(ident[:, :], 0.0).then_inc(ident_z, 1)
            pool.wait_ge(ident_z, 1)
            nc.gpsimd.affine_select(out=ident[:, :], in_=ident[:, :], compare_op=ALU.not_equal, fill=1.0, base=0,
                                    pattern=[[-1, P]], channel_multiplier=1).then_inc(ident_ok, 1)
            pool.wait_ge(ident_ok, 1)
            nc.gpsimd.tensor_copy(ident16[:, :], ident[:, :]).then_inc(ident_ok, 1)
            nc.gpsimd.memset(negsq[:, :].bitcast(F32), 0.0).then_inc(ident_ok, 1)

            pool.wait_ge(mv_ok, NR)
            pool.wait_ge(consts, 1)
            nc.gpsimd.tensor_scalar(vareps[:, :], meanvar[:, :, 1], EPS, 1.0, ALU.add, ALU.mult).then_inc(ln_step, 1)
            nc.gpsimd.tensor_scalar(negmean[:, :], meanvar[:, :, 0], -1.0, 0.0, ALU.mult, ALU.add).then_inc(ln_step, 1)
            pool.wait_ge(ln_step, 2)
            nc.gpsimd.tensor_tensor(rstd[:, :], vareps[:, :], neghalf[:, :], ALU.pow).then_inc(ln_step, 1)
            pool.wait_ge(ln_step, 3)
            nc.gpsimd.tensor_tensor(shift[:, :], negmean[:, :], rstd[:, :], ALU.mult).then_inc(ln_ok, 1)

            for R in range(NC):
                for J in range(1, NC):
                    n = R * NC + J
                    pool.wait_ge(summed, n + 1)
                    if J == 1 and R >= 2:
                        pool.wait_ge(deg_mm, R - 1)
                    if J > 1:
                        pool.wait_ge(added, adds(n))
                    nc.gpsimd.tensor_tensor(ut[:, R % 2, :], part[:, 0, :] if J == 1 else ut[:, R % 2, :],
                                            part[:, n % PARTS, :], ALU.add).then_inc(added, 1)
                pool.wait_ge(deg_ok, R + 1)
                c = slice(R * SUB, (R + 1) * SUB)
                nc.gpsimd.tensor_tensor(dis[:, c], deg[:, c], neghalf[:, c], ALU.pow).then_inc(dis_ok, 1)

            def stage_z(r, u):
                if not (static(r) and r < 2):
                    pool.wait_ge(zz_mm, r * 4 - 4)
                for i in range(2):
                    src = pan[i][:, r * P:(r + 1) * P] if static(r) else pan[i][:, ds(r * P, P)]
                    nc.gpsimd.tensor_copy(zslot[:, u % 2, i, :], src.bitcast(F32)).then_inc(zslot_ok, 1)

            def row(t, r):
                return t[:, r, :] if static(r) else t[:, ds(r, 1), :].rearrange("p a f -> p (a f)")

            def col(t, r):
                return t[:, r:r + 1] if static(r) else t[:, ds(r, 1)]

            def panel(t, r):
                return t[:, r * P:(r + 1) * P] if static(r) else t[:, ds(r * P, P)]

            def distances(r, u):
                pool.wait_ge(topi_ok, r + 1)
                nc.gpsimd.tensor_copy(row(idx, r), topi[:, u, 0:K]).then_inc(idx_ok, 1)
                nc.gpsimd.tensor_scalar(dist[:, u, 0, :], top[:, u, 0:K], -2.0, 0.0, ALU.mult, ALU.add).then_inc(dist_ok, 1)
                pool.wait_ge(dist_ok, r * 4 + 1)
                nc.gpsimd.tensor_tensor(dist[:, u, 1, :], dist[:, u, 0, :], col(sq, r).broadcast_to([P, K]),
                                        ALU.add).then_inc(dist_ok, 1)
                wait_apart(pool, dist_ok, r * 4 + 2)
                nc.gpsimd.tensor_scalar(dist[:, u, 2, :], dist[:, u, 1, :], 0.0, 1e-10, ALU.max, ALU.add).then_inc(dist_ok, 1)
                pool.wait_ge(dist_ok, r * 4 + 3)
                nc.gpsimd.tensor_tensor(dist[:, u, 3, :], dist[:, u, 2, :], poshalf[:, :], ALU.pow).then_inc(dist_ok, 1)
                pool.wait_ge(s4_ok, r + 1)
                nc.gpsimd.tensor_tensor(deg2[:, u:u + 1], ssum[:, u:u + 1], col(deg, r), ALU.add).then_inc(deg2_ok, 1)
                pool.wait_ge(deg2_ok, r + 1)
                nc.gpsimd.tensor_tensor(col(dis2, r), deg2[:, u:u + 1], neghalf[:, 0:1], ALU.pow).then_inc(dis2_ok, 1)
                pool.wait_ge(x2hi_ok, r + 1)
                nc.gpsimd.tensor_tensor(panel(x2p[1], r), x2s[:, u, :], panel(x2p[0], r).bitcast(F32),
                                        ALU.subtract).then_inc(x2lo_ok, 1)

            pool.wait_ge(zlo_ok, 1)
            stage_z(0, 0)
            stage_z(1, 1)
            stage_z(2, 0)
            pool.wait_ge(zlo_ok, NC)
            with pool.Fori(0, NR // GRP - 1) as it:
                for u in range(GRP):
                    stage_z(it * GRP + (u + 3), u + 1)
                    distances(it * GRP + u, u)
            for u in range(GRP):
                r = NR - GRP + u
                if r + 3 < NR:
                    stage_z(r + 3, u + 1)
                distances(r, u)

            def add_b2(c):
                pool.wait_ge(xb_in, c * 16 + 16)
                if not (static(c) and c == 0):
                    pool.wait_ge(x1_ok, c * SUB)
                nc.gpsimd.tensor_tensor(zt[:, 1, :, :], zt[:, 0, :, :],
                                        b2s[:, :].rearrange("p (a f) -> p a f", a=1).broadcast_to([P, SUB, D]),
                                        ALU.add).then_inc(xb_ok, 1)

            for half in range(2):
                pool.wait_ge(x2_out[half], 8 * NR)

            def gather(c, q):
                r, i = c * SUB + q, (c * SUB + q) % (2 * SUB)
                if c >= 2:
                    pool.wait_ge(weighed, (K - 1) * (r - 2 * SUB + 1))
                nc.gpsimd.tensor_copy(idxs[:, i, :], idx[:, r, :]).then_inc(idxs_ok, 1)
                pool.wait_ge(idxs_ok, r + 1)
                for k in range(K):
                    nc.gpsimd.indirect_dma_start(
                        out=xg(c, q, k), out_offset=None, in_=x2d[:, :],
                        in_offset=bass.IndirectOffsetOnAxis(ap=idxs[:, i, k:k + 1], axis=0),
                    ).then_inc(gathered[i], 16)

            def ln_factors(c):
                n = 5 * c
                pool.wait_ge(lnsc_ok, n + 2)
                nc.gpsimd.tensor_tensor(lnsc[:, 1, :], lnsc[:, 0, :], neghalf[:, 0:SUB], ALU.pow).then_inc(lnsc_ok, 1)
                pool.wait_ge(lnsc_ok, n + 3)
                nc.gpsimd.tensor_tensor(lnsc[:, 2, :], lnsc[:, 1, :], dis[:, c * SUB:(c + 1) * SUB],
                                        ALU.mult).then_inc(lnsc_ok, 1)
                pool.wait_ge(lnsc_ok, n + 4)
                nc.gpsimd.tensor_tensor(lnsc[:, 4, :], lnsc[:, 3, :], lnsc[:, 2, :], ALU.mult).then_inc(lnsc_ok, 1)
                if c + 1 < NC:
                    add_b2(c + 1)

            for c in range(NC):
                for q in range(SUB):
                    for ch in range(NC):
                        if LN_BEFORE[ch] == (c, q):
                            ln_factors(ch)
                    gather(c, q)
                if c == 0:
                    add_b2(0)
            for c in range(NC):
                if LN_BEFORE[c] is None:
                    ln_factors(c)

            def send(k, par):
                pool.wait_ge(y_ok, k * SUB + SUB)
                c = out_chunk(k)
                rows = slice(c * SUB, (c + 1) * SUB) if static(c) else ds(c * SUB, SUB)
                pool.dma_start(out[:, rows, :], h[:, rows, :]).then_inc(y_sent[par], 16)

            send(0, 0)
            send(1, 1)
            with pool.Fori(1, NC // 2) as it:
                for par in range(2):
                    send(it * 2 + par, par)


def kernel(x, adj, L0_gnn_W1, L0_gnn_b1, L0_gnn_W2, L0_gnn_b2, L1_gnn_weight):
    import numpy as np
    import concourse.bacc as bacc
    from concourse.bass_utils import run_bass_kernel_spmd as run

    xr = np.ascontiguousarray(np.asarray(x).reshape(NR, P, D).transpose(1, 0, 2))
    at = np.ascontiguousarray(np.asarray(adj).reshape(NC, CH, NC, SUB, P).transpose(0, 2, 4, 3, 1))
    arrays = {"in_x": xr, "in_at": at}
    for name, w in (("w1", L0_gnn_W1), ("b1", L0_gnn_b1), ("w2", L0_gnn_W2), ("b2", L0_gnn_b2), ("w3", L1_gnn_weight)):
        arrays["in_" + name] = np.ascontiguousarray(np.asarray(w))
    nc = bacc.Bacc("TRN2", target_bir_lowering=False, num_devices=1)
    ap = {n: nc.dram_tensor(n, a.shape, mybir.dt.from_np(a.dtype), kind="ExternalInput").ap() for n, a in arrays.items()}
    out = nc.dram_tensor("out_rows", (P, NR, D), F32, kind="ExternalOutput").ap()
    build(nc, ap["in_x"], ap["in_at"], ap["in_w1"], ap["in_b1"], ap["in_w2"], ap["in_b2"], ap["in_w3"], out)
    r = run(nc, [arrays], core_ids=[0])
    y = r.results[0]["out_rows"]
    return np.ascontiguousarray(y.transpose(1, 0, 2).reshape(N, D))
```
